# Optimizing a Trainium2 kernel written in Bass

```python
import numpy as np
import jax
import jax.numpy as jnp

def _softmax(x, axis=-1):
    return jax.nn.softmax(x, axis=axis)

def _gelu(x):
    return jax.nn.gelu(x, approximate=True)

def _silu(x):
    return jax.nn.silu(x)

def _sigmoid(x):
    return jax.nn.sigmoid(x)

def _layernorm(x, axis=-1, eps=1e-05):
    m = jnp.mean(x, axis=axis, keepdims=True)
    v = jnp.var(x, axis=axis, keepdims=True)
    return (x - m) / jnp.sqrt(v + eps)

def _scatter_add(tgt, idx, src, axis=0):
    return tgt.at[idx].add(src)

def _segment_sum(src, seg, n):
    return jax.ops.segment_sum(src, seg, n)
kernel_name = 'mk_adaln_d1_jaxref_r4_7d2e56'

def setup_inputs(seed: int=0):
    np.random.seed(seed)
    _w = jnp.asarray

    def _L0_attn_setup():
        import jax, jax.numpy as jnp
        import numpy as np
        B, L, HID = (1, 1024, 512)
        H, P, N, CH, K = (64, 64, 128, 64, 4)
        INTER = H * P
        CONV_DIM = INTER + 2 * N
        OUT_IN = 2 * (INTER + N) + H
        DT_MIN, DT_MAX, EPS = (0.0, 100.0, 1e-05)
        key = jax.random.key(seed)
        ks = jax.random.split(key, 6)
        hidden_states = jax.random.normal(ks[0], (B, L, HID), jnp.float32)
        W_in = jax.random.normal(ks[1], (HID, OUT_IN), jnp.float32) * 0.02
        conv_w = jax.random.normal(ks[2], (K, CONV_DIM), jnp.float32) * 0.1
        conv_b = jnp.zeros((CONV_DIM,), jnp.float32)
        u = jax.random.uniform(ks[3], (H,))
        dt = jnp.exp(u * (jnp.log(0.1) - jnp.log(0.001)) + jnp.log(0.001))
        dt_bias = dt + jnp.log(-jnp.expm1(-dt))
        A_log = jnp.log(jax.random.uniform(ks[4], (H,), minval=1.0, maxval=16.0))
        D = jnp.ones((H,), jnp.float32)
        norm_weight = jnp.ones((INTER,), jnp.float32)
        W_out = jax.random.normal(ks[5], (INTER, HID), jnp.float32) * 0.02
        return dict(hidden_states=hidden_states, W_in=W_in, conv_w=conv_w, conv_b=conv_b, dt_bias=dt_bias, A_log=A_log, D=D, norm_weight=norm_weight, W_out=W_out)
    _L0_attn_in = _L0_attn_setup()

    def _L0_ffn_setup():
        import jax, jax.numpy as jnp
        import numpy as np
        HIDDEN = 512
        INTER = 1408
        B, S = (2, 512)

        def _ternary(key, shape):
            return jax.random.randint(key, shape, -1, 2).astype(jnp.float32)
        key = jax.random.key(seed)
        ks = jax.random.split(key, 7)
        x = jax.random.normal(ks[0], (B, S, HIDDEN), dtype=jnp.float32)
        gate_w = _ternary(ks[1], (INTER, HIDDEN))
        up_w = _ternary(ks[2], (INTER, HIDDEN))
        down_w = _ternary(ks[3], (HIDDEN, INTER))
        gate_s = jax.random.uniform(ks[4], (INTER,), minval=0.01, maxval=0.1, dtype=jnp.float32)
        up_s = jax.random.uniform(ks[5], (INTER,), minval=0.01, maxval=0.1, dtype=jnp.float32)
        down_s = jax.random.uniform(ks[6], (HIDDEN,), minval=0.01, maxval=0.1, dtype=jnp.float32)
        return {'x': x, 'gate_w': gate_w, 'up_w': up_w, 'down_w': down_w, 'gate_s': gate_s, 'up_s': up_s, 'down_s': down_s}
    _L0_ffn_in = _L0_ffn_setup()
    _L0_c = _w((lambda *s: np.random.randn(*s).astype(np.float32) * 0.05)(1, 512))
    _L0_wmod = _w((lambda *s: np.random.randn(*s).astype(np.float32) * 0.05)(512, 6 * 512) * 512 ** (-0.5))
    _d = {'L0_attn_hidden_states': _L0_attn_in['hidden_states'], 'L0_attn_W_in': _L0_attn_in['W_in'], 'L0_attn_conv_w': _L0_attn_in['conv_w'], 'L0_attn_conv_b': _L0_attn_in['conv_b'], 'L0_attn_dt_bias': _L0_attn_in['dt_bias'], 'L0_attn_A_log': _L0_attn_in['A_log'], 'L0_attn_D': _L0_attn_in['D'], 'L0_attn_norm_weight': _L0_attn_in['norm_weight'], 'L0_attn_W_out': _L0_attn_in['W_out'], 'L0_ffn_gate_w': _L0_ffn_in['gate_w'], 'L0_ffn_up_w': _L0_ffn_in['up_w'], 'L0_ffn_down_w': _L0_ffn_in['down_w'], 'L0_ffn_gate_s': _L0_ffn_in['gate_s'], 'L0_ffn_up_s': _L0_ffn_in['up_s'], 'L0_ffn_down_s': _L0_ffn_in['down_s'], 'L0_c': _L0_c, 'L0_wmod': _L0_wmod}
    _x0 = _d['L0_attn_hidden_states']
    _d['L0_attn_hidden_states'] = jax.random.normal(jax.random.fold_in(jax.random.key(seed), 1), (1, 2048, 512), dtype=_x0.dtype)
    del _x0
    return _d

def reference(L0_attn_hidden_states, L0_attn_W_in, L0_attn_conv_w, L0_attn_conv_b, L0_attn_dt_bias, L0_attn_A_log, L0_attn_D, L0_attn_norm_weight, L0_attn_W_out, L0_ffn_gate_w, L0_ffn_up_w, L0_ffn_down_w, L0_ffn_gate_s, L0_ffn_up_s, L0_ffn_down_s, L0_c, L0_wmod):

    def _L0_attn_ref(hidden_states, W_in, conv_w, conv_b, dt_bias, A_log, D, norm_weight, W_out):
        import jax, jax.numpy as jnp
        import numpy as np
        B, L, HID = (1, 1024, 512)
        H, P, N, CH, K = (64, 64, 128, 64, 4)
        INTER = H * P
        CONV_DIM = INTER + 2 * N
        OUT_IN = 2 * (INTER + N) + H
        DT_MIN, DT_MAX, EPS = (0.0, 100.0, 1e-05)
        Bsz, Ls, _ = hidden_states.shape
        nc = Ls // CH
        zxbcdt = hidden_states @ W_in
        z, xBC, dt = jnp.split(zxbcdt, [INTER, 2 * INTER + 2 * N], axis=-1)
        xp = jnp.pad(xBC, ((0, 0), (K - 1, 0), (0, 0)))
        xBC = sum((xp[:, k:k + Ls, :] * conv_w[k] for k in range(K))) + conv_b
        xBC = jax.nn.silu(xBC)
        x, Bt, Ct = jnp.split(xBC, [INTER, INTER + N], axis=-1)
        x = x.reshape(Bsz, Ls, H, P)
        dt = jnp.clip(jax.nn.softplus(dt + dt_bias), DT_MIN, DT_MAX)
        A = -jnp.exp(A_log)
        xc = x.reshape(Bsz, nc, CH, H, P)
        Bc = Bt.reshape(Bsz, nc, CH, N)
        Cc = Ct.reshape(Bsz, nc, CH, N)
        dtc = dt.reshape(Bsz, nc, CH, H)
        xdt = xc * dtc[..., None]
        dA = jnp.transpose(dtc * A, (0, 3, 1, 2))
        A_cs = jnp.cumsum(dA, axis=-1)
        seg = A_cs[..., :, None] - A_cs[..., None, :]
        tri = jnp.tril(jnp.ones((CH, CH), bool))
        Lmat = jnp.where(tri, jnp.exp(seg), 0.0)
        Y_diag = jnp.einsum('bcln,bcsn,bhcls,bcshp->bclhp', Cc, Bc, Lmat, xdt)
        decay_states = jnp.exp(A_cs[..., -1:] - A_cs)
        states = jnp.einsum('bcln,bhcl,bclhp->bchpn', Bc, decay_states, xdt)
        chunk_end = A_cs[..., -1]
        pad_cs = jnp.pad(jnp.cumsum(chunk_end, axis=-1), ((0, 0), (0, 0), (1, 0)))
        segc = pad_cs[..., :, None] - pad_cs[..., None, :]
        tric = jnp.tril(jnp.ones((nc + 1, nc + 1), bool))
        decay_chunk = jnp.where(tric, jnp.exp(segc), 0.0)
        init = jnp.zeros((Bsz, 1, H, P, N), states.dtype)
        states = jnp.concatenate([init, states], axis=1)
        new_states = jnp.einsum('bhzc,bchpn->bzhpn', decay_chunk, states)
        states_in = new_states[:, :-1]
        state_decay = jnp.exp(A_cs)
        Y_off = jnp.einsum('bcln,bchpn,bhcl->bclhp', Cc, states_in, state_decay)
        y = (Y_diag + Y_off).reshape(Bsz, Ls, H, P)
        y = y + x * D[None, None, :, None]
        y = y.reshape(Bsz, Ls, INTER)
        yf = y.astype(jnp.float32) * jax.nn.silu(z.astype(jnp.float32))
        var = jnp.mean(yf * yf, axis=-1, keepdims=True)
        yf = yf * jax.lax.rsqrt(var + EPS) * norm_weight
        y = yf.astype(hidden_states.dtype)
        return y @ W_out

    def _L0_ffn_ref(x, gate_w, up_w, down_w, gate_s, up_s, down_s):
        import jax, jax.numpy as jnp
        import numpy as np
        HIDDEN = 512
        INTER = 1408
        B, S = (2, 512)

        def _ternary(key, shape):
            return jax.random.randint(key, shape, -1, 2).astype(jnp.float32)
        b, s, h = x.shape
        xf = x.reshape(b * s, h)
        g = jnp.einsum('th,ih->ti', xf, gate_w) * gate_s
        u = jnp.einsum('th,ih->ti', xf, up_w) * up_s
        hdn = jax.nn.silu(g) * u
        out = jnp.einsum('ti,hi->th', hdn, down_w) * down_s
        return out.reshape(b, s, -1)
    x = L0_attn_hidden_states
    mod = (_silu(L0_c) @ L0_wmod).reshape(L0_c.shape[0], 6, 1, -1)
    sa, ca, ga, sb, cb, gb = (mod[:, 0], mod[:, 1], mod[:, 2], mod[:, 3], mod[:, 4], mod[:, 5])
    ga = (2 * (ga >= 0) - 1) * jnp.maximum(jnp.abs(ga), 0.25)
    gb = (2 * (gb >= 0) - 1) * jnp.maximum(jnp.abs(gb), 0.25)
    h = _layernorm(x, axis=-1) * (1 + ca) + sa
    x = x + ga * _L0_attn_ref(h, L0_attn_W_in, L0_attn_conv_w, L0_attn_conv_b, L0_attn_dt_bias, L0_attn_A_log, L0_attn_D, L0_attn_norm_weight, L0_attn_W_out)
    h = _layernorm(x, axis=-1) * (1 + cb) + sb
    x = x + gb * _L0_ffn_ref(h, L0_ffn_gate_w, L0_ffn_up_w, L0_ffn_down_w, L0_ffn_gate_s, L0_ffn_up_s, L0_ffn_down_s)
    return x

_drawn_inputs = setup_inputs


def setup_inputs(seed=0):
    import zlib

    import numpy as np

    out = dict(_drawn_inputs(seed))
    spreads = {'L0_attn_conv_b': (0.0, 0.1), 'L0_attn_D': (1.0, 0.2), 'L0_attn_norm_weight': (1.0, 0.2)}
    factors = {}
    for name, (base, spread) in spreads.items():
        noise = np.random.default_rng([zlib.crc32(name.encode()), seed]).standard_normal(out[name].shape)
        drawn = base * np.exp(spread * noise) if base else spread * noise
        out[name] = jnp.asarray(drawn.astype(out[name].dtype))
    for name, factor in factors.items():
        out[name] = (out[name] * factor).astype(out[name].dtype)
    return out
```

```python
from contextlib import ExitStack

import numpy as np

import concourse.bass as bass
from concourse import mybir

F32 = mybir.dt.float32
F32R = mybir.dt.float32r
ALU = mybir.AluOpType
ACT = mybir.ActivationFunctionType

P = 128
TOKENS, HID = 2048, 512
HEADS, HEAD_P, STATE = 64, 64, 128
INTER = HEADS * HEAD_P
KT = HID // P
HALVES = 2
TH = TOKENS // HALVES
NB = TH // P
BANKS = TH // 512
PAIRS = INTER // P
TILES = PAIRS + 2
TAPS = 4
FFN = 1408
FT = FFN // P
LN_EPS = RMS_EPS = 1e-5
DT_MAX = 100.0
EDGES = 5
ENGINES = 5
START = 1

DVE_STEPS = dict(setup=14, half=779, pair=21, ffn=1)


class Steps:

    def __init__(self, engine, sem):
        self.engine, self.sem, self.base, self.count = engine, sem, 0, 0

    def mark(self, ins):
        ins.then_inc(self.sem, 1)
        self.count += 1

    def sync(self):
        self.engine.wait_ge(self.sem, self.base + self.count)

    def link(self, ins):
        self.mark(ins)
        self.sync()


class Semaphores:

    def __init__(self, sem):
        self.edge = sem("edge")
        self.passed = sem("passed")
        self.const_in = sem("const_in")
        self.const_ok = sem("const_ok")
        self.dve_step = sem("dve_step")
        self.wm_in = sem("wm_in")
        self.wm_used = sem("wm_used")
        self.mod_c = sem("mod_c")
        self.mod_s = sem("mod_s")
        self.mod_sb = sem("mod_sb")
        self.x_in = sem("x_in")
        self.xn = sem("xn")
        self.tp = sem("tp")
        self.h32 = sem("h32")
        self.ht = sem("ht")
        self.wdt_hi = sem("wdt_hi")
        self.wdt_lo = sem("wdt_lo")
        self.dt_mm = sem("dt_mm")
        self.dt_abs = sem("dt_abs")
        self.dt_exp = sem("dt_exp")
        self.dt_u = sem("dt_u")
        self.dt_ln = sem("dt_ln")
        self.dta = sem("dta")
        self.cs_mm = sem("cs_mm")
        self.cs_sb = sem("cs_sb")
        self.csm = sem("csm")
        self.dec = sem("dec")
        self.cs_tp = sem("cs_tp")
        self.cs_row_ok = sem("cs_row_ok")
        self.scratch = sem("scratch")
        self.cb_mm = sem("cb_mm")
        self.cb_ok = sem("cb_ok")
        self.btok_tp = sem("btok_tp")
        self.btok = sem("btok")
        self.wx_in = sem("wx_in")
        self.wx_hi = sem("wx_hi")
        self.wx_lo = sem("wx_lo")
        self.wz_in = sem("wz_in")
        self.wz_hi = sem("wz_hi")
        self.wz_lo = sem("wz_lo")
        self.wo_in = sem("wo_in")
        self.wo_wn = sem("wo_wn")
        self.wo_hi = sem("wo_hi")
        self.wo_lo = sem("wo_lo")
        self.xp = sem("xp")
        self.halo_in = sem("halo_in")
        self.xev = sem("xev")
        self.tap0 = sem("tap0")
        self.taps = sem("taps")
        self.thc = sem("thc")
        self.xs = sem("xs")
        self.zp = sem("zp")
        self.thz = sem("thz")
        self.szr = sem("szr")
        self.xT = sem("xT")
        self.xdt_r = sem("xdt_r")
        self.xd_r = sem("xd_r")
        self.st = sem("st")
        self.sin = sem("sin")
        self.erow_in = sem("erow_in")
        self.seg = sem("seg")
        self.seg_min = sem("seg_min")
        self.ex = sem("ex")
        self.mt_r = sem("mt_r")
        self.yp = sem("yp")
        self.y_read = sem("y_read")
        self.g_r = sem("g_r")
        self.ghi = sem("ghi")
        self.glo = sem("glo")
        self.sqr = sem("sqr")
        self.ssq = sem("ssq")
        self.op = sem("op")
        self.oacc = sem("oacc")
        self.ss_mm = sem("ss_mm")
        self.x2 = sem("x2")
        self.var_r = sem("var_r")
        self.root_r = sem("root_r")
        self.wg_in = sem("wg_in")
        self.wg_hi = sem("wg_hi")
        self.wg_lo = sem("wg_lo")
        self.wu_in = sem("wu_in")
        self.wu_hi = sem("wu_hi")
        self.wu_lo = sem("wu_lo")
        self.wd_in = sem("wd_in")
        self.wd_hi = sem("wd_hi")
        self.wd_lo = sem("wd_lo")
        self.gp = sem("gp")
        self.up = sem("up")
        self.gh = sem("gh")
        self.thg = sem("thg")
        self.hd = sem("hd")
        self.hdhi = sem("hdhi")
        self.hdlo = sem("hdlo")
        self.fp = sem("fp")
        self.facc = sem("facc")
        self.fin = sem("fin")
        self.out_ok = sem("out_ok")
        self.xres_in = [sem(f"xres_in{k}") for k in range(2)]
        self.csrow_in = [sem(f"csrow_in{k}") for k in range(2)]


def build(nc, a, out):
    ctx = ExitStack()
    with ctx:
        def sb(name, shape, dt=F32):
            return ctx.enter_context(nc.sbuf_tensor(name, shape, dt))

        def ps(name, shape):
            return ctx.enter_context(nc.psum_tensor(name, shape, F32))

        def sem(name):
            return ctx.enter_context(nc.semaphore(name))

        ident = sb("ident", [P, P])
        tri = sb("tri", [P, P])
        ones = sb("ones", [P, P])
        c_col = sb("c_col", [P, KT])
        c_half = sb("c_half", [P, KT])
        c_tanh = sb("c_tanh", [P, KT])
        c_silu = sb("c_silu", [P, KT])
        mod_col = sb("mod_col", [P, 4, KT])
        gate_a = sb("gate_a", [P, HID])
        gate_b = sb("gate_b", [P, HID])
        conv_w = sb("conv_w", [P, TILES, TAPS])
        conv_b = sb("conv_b", [P, TILES])
        d_col = sb("d_col", [P, PAIRS])
        norm_col = sb("norm_col", [P, PAIRS])
        ffn_gs = sb("ffn_gs", [P, FT])
        ffn_us = sb("ffn_us", [P, FT])
        dt_bias = sb("dt_bias", [P, HEADS])
        exp_a = sb("exp_a", [P, HEADS])
        ht_hi = sb("ht_hi", [P, KT, TH], F32R)
        ht_lo = sb("ht_lo", [P, KT, TH], F32R)
        acc = sb("acc", [P, NB, HID])
        c_t = sb("c_t", [P, TH])
        b_tok = sb("b_tok", [P, NB, STATE])
        cb = sb("cb", [P, NB, P])
        dt = sb("dt", [P, NB, HEADS])
        cs = sb("cs", [P, NB, HEADS])
        dt_end = sb("dt_end", [P, NB, HEADS])
        e_last = sb("e_last", [P, NB, HEADS])
        halo = sb("halo", [P, TILES, TAPS - 1])
        carry = sb("carry", [P, PAIRS, P])
        sumsq = sb("sumsq", [P, TH])
        big = sb("big", [P, 4, TH])
        cs_row, mt = big[:, 0:2, :], big[:, 2:4, :]
        e_row = sb("e_row", [P, TH])
        xraw = sb("xraw", [P, TAPS - 1 + TH])
        conv = sb("conv", [P, TH])
        conv_th = sb("conv_th", [P, TH])
        xs = sb("xs", [P, TH])
        z_th = sb("z_th", [P, TH])
        sz = sb("sz", [P, TH])
        xdt = sb("xdt", [P, NB, P])
        xd = sb("xd", [P, NB, P])
        s_in = sb("s_in", [P, NB, P])
        g = sb("g", [P, TH])
        g_hi = sb("g_hi", [P, TH], F32R)
        g_lo = sb("g_lo", [P, TH], F32R)
        sq = sb("sq", [P, TH])
        w_raw = sb("w_raw", [P, 3, 512])
        w_hi = sb("w_hi", [P, 3, 512], F32R)
        w_lo = sb("w_lo", [P, 3, 512], F32R)
        X, Z, O = 0, 1, 2
        wdt_raw = sb("wdt_raw", [P, KT, HEADS])
        wdt_hi = sb("wdt_hi", [P, KT, HEADS], F32R)
        wdt_lo = sb("wdt_lo", [P, KT, HEADS], F32R)
        stat = sb("stat", [P, NB, 6])
        mv = sb("mv", [P, NB, 2])
        var = sb("var", [P, NB])
        root = sb("root", [P, NB])
        rstd = sb("rstd", [P, NB])
        xn = conv_th[:, :].rearrange("p (u n) -> p u n", u=2)
        h32 = z_th[:, :].rearrange("p (u k t) -> p u k t", u=2, k=KT)
        b_t = sz
        cs_t, ecs_t = xdt[0:HEADS], xd[0:HEADS]
        f_acc = big[:, :, :].rearrange("p a (b n) -> p (a b) n", n=HID)
        wmod_sb = big[:, 0:2, :].rearrange("p a (b n) -> p (a b) n", n=HID)

        psx = ps("psx", [P, BANKS, 512])
        pst = ps("pst", [P, BANKS, 512])
        psy = ps("psy", [P, 2, 512])
        pso = ps("pso", [P, 2, 512])
        pst_b = pst[:, :, :].rearrange("p a (b n) -> p (a b) n", n=P)

        s = Semaphores(sem)

        scr_cs = nc.dram_tensor("scr_cs", (HALVES, HEADS, TH), F32).ap()
        scr_ecs = nc.dram_tensor("scr_ecs", (HALVES, HEADS, TH), F32).ap()
        x_v = a["x"].rearrange("(h b p) n -> h b p n", h=HALVES, p=P)
        out_v = out.rearrange("(h b p) n -> h b p n", h=HALVES, p=P)
        wmod_v = a["wmod"].rearrange("(k p) (m n) -> m p k n", p=P, n=HID)

        def wait_alone(e, which, value):
            e.wait_ge(which, value)
            e.sem_inc(s.passed, 1)

        def start_counters(e, *counters):
            for counter in counters:
                e.sem_inc(counter, START)

        def edge(e, h, k):
            e.drain().then_inc(s.edge, 1)
            wait_alone(e, s.edge, (h * EDGES + k) * ENGINES)

        def mm3(e, dst, w_h, w_l, m_h, m_l, start, stop):
            e.matmul(dst, w_h, m_h, start=start, stop=False)
            e.matmul(dst, w_h, m_l, start=False, stop=False)
            return e.matmul(dst, w_l, m_h, start=False, stop=stop)

        block = ctx.enter_context(nc.Block())

        @block.sync
        def _(e):
            consts = [
                (c_col[:, :], a["c"]), (conv_w[:, :, :], a["conv_w"]), (conv_b[:, :], a["conv_b"]),
                (norm_col[:, :], a["norm_w"]), (ffn_gs[:, :], a["gate_s"]), (ffn_us[:, :], a["up_s"]),
                (wdt_raw[:, :, :], a["wdt"]),
                (dt_bias[:, :], a["dt_bias"].partition_broadcast(P)),
                (exp_a[:, :], a["a_log"].partition_broadcast(P)),
                (d_col[0:HEAD_P, :], a["d"][0].partition_broadcast(HEAD_P)),
                (d_col[HEAD_P:P, :], a["d"][1].partition_broadcast(HEAD_P)),
                (g[:, 0:HID], a["down_s"].partition_broadcast(P)),
            ]
            for dst, src in consts:
                e.dma_start(dst, src).then_inc(s.const_in, 16)
            for m in range(6):
                if m:
                    e.wait_ge(s.wm_used, m)
                e.dma_start(wmod_sb, wmod_v[m]).then_inc(s.wm_in, 16)
            with e.Fori(0, HALVES) as h:
                edge(e, h, 1)
                e.dma_start(acc[:, :, :], x_v[h].rearrange("b p n -> p b n")).then_inc(s.x_in, 16)
                e.dma_start(w_raw[:, X, :], a["wx"][0]).then_inc(s.wx_in, 16)
                edge(e, h, 2)
                e.dma_start(w_raw[:, Z, :], a["wz"][0]).then_inc(s.wz_in, 16)
                e.dma_start(w_raw[:, O, :], a["wo"][0]).then_inc(s.wo_in, 16)

                def load_x(j):
                    e.wait_ge(s.wx_lo, START + h * TILES + j)
                    e.dma_start(w_raw[:, X, :], a["wx"][j]).then_inc(s.wx_in, 16)

                def load_z(i):
                    e.wait_ge(s.wz_lo, START + h * PAIRS + i)
                    e.dma_start(w_raw[:, Z, :], a["wz"][i]).then_inc(s.wz_in, 16)

                def load_o(i):
                    e.wait_ge(s.wo_lo, START + h * PAIRS + i)
                    e.dma_start(w_raw[:, O, :], a["wo"][i]).then_inc(s.wo_in, 16)

                def load_cs(i):
                    e.wait_ge(s.seg, START + 2 * (h * PAIRS + i))
                    for r in range(2):
                        e.dma_start(cs_row[:, r, :], scr_cs[h, 2 * i + r].partition_broadcast(P)) \
                            .then_inc(s.csrow_in[r], 16)

                def load_e(i):
                    e.wait_ge(s.y_read, START + 2 * (h * PAIRS + i))
                    for r in range(2):
                        e.dma_start(e_row[r * HEAD_P:(r + 1) * HEAD_P, :],
                                    scr_ecs[h, 2 * i + r].partition_broadcast(HEAD_P)) \
                            .then_inc(s.erow_in, 16)

                load_x(1)
                load_x(2)
                e.wait_ge(s.cs_row_ok, 2 * (h + 1))
                e.dma_start(scr_cs[h], cs_t.rearrange("p b t -> p (b t)")).then_inc(s.scratch, 16)
                e.dma_start(scr_ecs[h], ecs_t.rearrange("p b t -> p (b t)")).then_inc(s.scratch, 16)
                e.wait_ge(s.scratch, 32 * (h + 1))
                load_cs(0)
                load_e(0)
                load_x(3)
                load_z(1)
                edge(e, h, 3)
                with e.Fori(0, PAIRS - 2) as i:
                    load_cs(i + 1)
                    load_x(i + 4)
                    load_z(i + 2)
                    load_o(i + 1)
                    load_e(i + 1)
                load_cs(PAIRS - 1)
                load_o(PAIRS - 1)
                load_e(PAIRS - 1)
                edge(e, h, 4)
                for b in range(NB):
                    if b >= 2:
                        e.wait_ge(s.x2, h * NB + b - 1)
                    e.dma_start(sq[:, (b % 2) * HID:(b % 2 + 1) * HID], x_v[h, b]).then_inc(s.xres_in[b % 2], 16)
                n = h * FT
                for k, (src, done) in enumerate(((a["wu"], s.wu_in), (a["wg"], s.wg_in), (a["wd"], s.wd_in))):
                    e.dma_start(w_raw[:, k, :], src[0]).then_inc(done, 16)
                edge(e, h, 5)
                with e.Fori(0, FT - 1) as t:
                    for k, (src, used, done) in enumerate(((a["wu"], s.wu_lo, s.wu_in), (a["wg"], s.wg_lo, s.wg_in),
                                                           (a["wd"], s.wd_lo, s.wd_in))):
                        e.wait_ge(used, h * FT + t + 1)
                        e.dma_start(w_raw[:, k, :], src[t + 1]).then_inc(done, 16)
                for b in range(NB):
                    e.wait_ge(s.fin, h * NB + b + 1)
                    e.dma_start(out_v[h, b], acc[:, b, :]).then_inc(s.out_ok, 16)
                wait_alone(e, s.out_ok, 16 * NB * (h + 1))

        @block.scalar
        def _(e):
            start_counters(e, s.gh)
            def copy(o, i, **kw):
                return e.activation(o, i, ACT.Copy, **kw)

            e.wait_ge(s.const_in, 16 * 12)
            e.activation(c_half[:, :], c_col[:, :], ACT.Copy, scale=0.5).then_inc(s.mod_c, 1)
            e.activation(c_tanh[:, :], c_col[:, :], ACT.Tanh, scale=0.5).then_inc(s.mod_c, 1)
            e.activation(exp_a[:, :], exp_a[:, :], ACT.Exp).then_inc(s.mod_c, 1)
            copy(wdt_hi[:, :, :], wdt_raw[:, :, :]).then_inc(s.wdt_hi, 1)
            with e.Fori(0, HALVES) as h:
                edge(e, h, 1)

                def square_root(k):
                    e.wait_ge(s.var_r, 3 * h + k + 1)
                    e.activation(root[:, :], var[:, :], ACT.Sqrt).then_inc(s.root_r, 1)

                def transposed_norm(which):
                    for b in range(NB):
                        n = (2 * h + which) * NB + b
                        e.wait_ge(s.tp, n + 1)
                        if b >= 2:
                            e.wait_ge(s.ht, n - 1)
                        for k in range(KT):
                            ins = e.activation(h32[:, b % 2, k, :], pst[:, b % 2, k * P:(k + 1) * P], ACT.Identity,
                                               scale=mod_col[:, 2 * which + 1, k:k + 1],
                                               bias=mod_col[:, 2 * which, k:k + 1])
                        ins.then_inc(s.h32, 1)

                square_root(0)
                transposed_norm(0)
                edge(e, h, 2)

                def split_x(j):
                    m = h * TILES + j
                    e.wait_ge(s.wx_in, 16 * (m + 1))
                    e.wait_ge(s.xp, START + 2 * m)
                    copy(w_hi[:, X, :], w_raw[:, X, :]).then_inc(s.wx_hi, 1)

                def split_z(i):
                    n = h * PAIRS + i
                    e.wait_ge(s.wz_in, 16 * (n + 1))
                    e.wait_ge(s.zp, START + 2 * n)
                    copy(w_hi[:, Z, :], w_raw[:, Z, :]).then_inc(s.wz_hi, 1)

                def split_o(i):
                    n = h * PAIRS + i
                    e.wait_ge(s.wo_in, 16 * (n + 1))
                    e.activation(w_raw[:, O, :], w_raw[:, O, :], ACT.Copy,
                                 scale=norm_col[:, bass.ds(i, 1)]).then_inc(s.wo_wn, 1)
                    e.wait_ge(s.wo_wn, n + 1)
                    e.wait_ge(s.op, START + NB * n)
                    copy(w_hi[:, O, :], w_raw[:, O, :]).then_inc(s.wo_hi, 1)

                def evacuate_x(j, q):
                    m = h * TILES + j
                    e.wait_ge(s.xp, START + 2 * m + q + 1)
                    if q == 0:
                        e.wait_ge(s.taps, START + m)
                        copy(xraw[:, 0:TAPS - 1], halo[:, bass.ds(j, 1), :].rearrange("p a k -> p (a k)")) \
                            .then_inc(s.halo_in, 1)
                    c0 = TAPS - 1 + q * 512
                    copy(xraw[:, c0:c0 + 512], psx[:, q, :]).then_inc(s.xev, 1)

                def convolve(j):
                    m = h * TILES + j
                    e.wait_ge(s.xev, 2 * (m + 1))
                    e.wait_ge(s.halo_in, m + 1)
                    e.wait_ge(s.xs, START + m)
                    e.activation(conv[:, :], xraw[:, TAPS - 1:TAPS - 1 + TH], ACT.Identity,
                                 scale=conv_w[:, bass.ds(j, 1), TAPS - 1:TAPS].rearrange("p a k -> p (a k)"),
                                 bias=conv_b[:, bass.ds(j, 1)]).then_inc(s.tap0, 1)
                    copy(halo[:, bass.ds(j, 1), :].rearrange("p a k -> p (a k)"), xraw[:, TH:TH + TAPS - 1])
                    e.wait_ge(s.taps, START + m + 1)
                    e.activation(conv_th[:, :], conv[:, :], ACT.Tanh).then_inc(s.thc, 1)

                split_x(0)
                for q in range(2):
                    evacuate_x(0, q)
                convolve(0)
                split_x(1)
                for q in range(2):
                    evacuate_x(1, q)
                convolve(1)
                split_x(2)
                split_z(0)
                for q in range(2):
                    evacuate_x(2, q)
                e.wait_ge(s.dt_abs, h + 1)
                e.activation(conv_th[:, 512:1024], conv_th[:, 0:512], ACT.Exp, scale=-1.0).then_inc(s.dt_exp, 1)
                e.wait_ge(s.dt_u, h + 1)
                e.activation(z_th[:, 512:1024], z_th[:, 0:512], ACT.Ln).then_inc(s.dt_ln, 1)
                e.wait_ge(s.csm, h + 1)
                flat = lambda t: t[:, :, :].rearrange("p b k -> p (b k)")
                e.activation(flat(dt_end), flat(dt_end), ACT.Exp).then_inc(s.dec, 1)
                e.activation(flat(e_last), psy[:, 1, :], ACT.Exp).then_inc(s.dec, 1)
                e.wait_ge(s.cs_tp, h + 1)
                copy(cs_t.rearrange("p b t -> p (b t)"), pst[0:HEADS, :, :].rearrange("p a n -> p (a n)")) \
                    .then_inc(s.cs_row_ok, 1)
                e.activation(ecs_t.rearrange("p b t -> p (b t)"), pst[0:HEADS, :, :].rearrange("p a n -> p (a n)"),
                             ACT.Exp).then_inc(s.cs_row_ok, 1)
                edge(e, h, 3)

                def pair(i, last):
                    n = h * PAIRS + i
                    if not last:
                        split_x(i + 3)
                    convolve(i + 2)
                    e.wait_ge(s.zp, START + 2 * n + 2)
                    e.wait_ge(s.szr, START + n)
                    e.activation(z_th[:, :], psx[:, :, :].rearrange("p a n -> p (a n)"), ACT.Tanh, scale=0.5) \
                        .then_inc(s.thz, 1)
                    for r in range(2):
                        e.wait_ge(s.seg_min, n + 1)
                        e.activation(mt[:, r, :], mt[:, r, :], ACT.Exp).then_inc(s.ex, 1)
                    if not last:
                        split_z(i + 1)
                    split_o(i)
                    for q in range(2):
                        e.wait_ge(s.g_r, 2 * n + q + 1)
                        c = slice(q * 512, q * 512 + 512)
                        e.wait_ge(s.ssq, START + 2 * n + q)
                        e.wait_ge(s.op, START + NB * n)
                        copy(g_hi[:, c], g[:, c]).then_inc(s.ghi, 1)
                        e.activation(sq[:, c], g[:, c], ACT.Square).then_inc(s.sqr, 1)
                        if not last:
                            evacuate_x(i + 3, q)

                with e.Fori(0, PAIRS - 1) as i:
                    pair(i, False)
                pair(PAIRS - 1, True)
                edge(e, h, 4)
                square_root(1)
                square_root(2)
                transposed_norm(1)
                edge(e, h, 5)

                def ffn(t):
                    n = h * FT + t
                    def split(k, here, used, before, done):
                        e.wait_ge(here, 16 * (n + 1))
                        e.wait_ge(used, START + before)
                        copy(w_hi[:, k, :], w_raw[:, k, :]).then_inc(done, 1)

                    split(Z, s.wg_in, s.gp, n, s.wg_hi)
                    split(X, s.wu_in, s.up, n, s.wu_hi)
                    e.wait_ge(s.gp, START + n + 1)
                    e.wait_ge(s.hd, START + n)
                    e.activation(conv[:, :], psx[:, :, :].rearrange("p a n -> p (a n)"), ACT.Copy,
                                 scale=ffn_gs[:, bass.ds(t, 1)]).then_inc(s.gh, 1)
                    e.wait_ge(s.gh, START + n + 1)
                    e.activation(conv_th[:, :], conv[:, :], ACT.Tanh).then_inc(s.thg, 1)
                    split(O, s.wd_in, s.fp, NB * n, s.wd_hi)
                    e.wait_ge(s.hd, START + n + 1)
                    e.wait_ge(s.fp, START + NB * n)
                    copy(g_hi[:, :], g[:, :]).then_inc(s.hdhi, 1)

                with e.Fori(0, FT) as t:
                    ffn(t)

        @block.tensor
        def _(e):
            start_counters(e, s.xp, s.zp, s.op, s.fp, s.yp, s.gp, s.up)
            e.wait_ge(s.const_ok, 5)
            e.wait_ge(s.mod_s, 1)
            for m in range(6):
                e.wait_ge(s.wm_in, 16 * (m + 1))
                if m in (2, 5):
                    e.wait_ge(s.mod_sb, 1)
                    for k in range(KT):
                        ins = e.matmul(pso[:, m // 3, :], xdt[:, k, :], wmod_sb[:, k, :],
                                       start=k == 0, stop=k == KT - 1)
                else:
                    for j in range(KT):
                        col = (m if m < 2 else m - 1) * KT + j
                        for k in range(KT):
                            ins = e.matmul(psy[:, 0, col:col + 1], wmod_sb[:, k, j * P:(j + 1) * P],
                                           c_silu[:, k:k + 1], start=k == 0, stop=k == KT - 1)
                ins.then_inc(s.wm_used, 1)
            with e.Fori(0, HALVES) as h:
                edge(e, h, 1)

                def transpose_norm(which):
                    for b in range(NB):
                        n = (2 * h + which) * NB + b
                        e.wait_ge(s.xn, n + 1)
                        if b >= 2:
                            e.wait_ge(s.h32, n - 1)
                        for k in range(KT):
                            ins = e.transpose(pst[:, b % 2, k * P:(k + 1) * P], xn[:, b % 2, k * P:(k + 1) * P],
                                              ident[:, :])
                        ins.then_inc(s.tp, 1)

                def project(dst, w, q, done):
                    for k in range(KT):
                        c, t = slice(k * P, (k + 1) * P), slice(q * 512, (q + 1) * 512)
                        ins = mm3(e, dst, w_hi[:, w, c], w_lo[:, w, c], ht_hi[:, k, t], ht_lo[:, k, t],
                                  k == 0, k == KT - 1)
                    if done is not None:
                        ins.then_inc(done, 1)
                    return ins

                def project_x(j, q):
                    if q == 0:
                        e.wait_ge(s.wx_lo, START + h * TILES + j + 1)
                    project(psx[:, q, :], X, q, s.xp)

                transpose_norm(0)
                edge(e, h, 2)
                for j in range(3):
                    for q in range(2):
                        if j:
                            e.wait_ge(s.xev, 2 * (h * TILES + j) + q - 1)
                        project_x(j, q)
                    if j == 0:
                        e.wait_ge(s.wdt_lo, 1)
                        for b in range(NB):
                            t = slice(b * P, (b + 1) * P)
                            for k in range(KT):
                                ins = mm3(e, psy[:, 0, b * HEADS:(b + 1) * HEADS], ht_hi[:, k, t], ht_lo[:, k, t],
                                          wdt_hi[:, k, :], wdt_lo[:, k, :], k == 0, k == KT - 1)
                        ins.then_inc(s.dt_mm, 1)
                e.wait_ge(s.xs, START + h * TILES + 1)
                for b in range(NB):
                    ins = e.transpose(pst_b[:, b, :], b_t[:, b * P:(b + 1) * P], ident[:, :])
                ins.then_inc(s.btok_tp, 1)
                e.wait_ge(s.xs, START + h * TILES + 2)
                e.wait_ge(s.btok, h + 1)
                for b in range(NB):
                    t = slice(b * P, (b + 1) * P)
                    ins = e.matmul(pst_b[:, b, :], b_t[:, t], c_t[:, t], start=True, stop=True)
                ins.then_inc(s.cb_mm, 1)
                e.wait_ge(s.dta, h + 1)
                flat = lambda t: t[:, :, :].rearrange("p b k -> p (b k)")
                e.matmul(psy[:, 0, :], tri[:, :], flat(dt_end), start=True, stop=True)
                e.matmul(psy[:, 1, :], ones[:, :], flat(dt_end), start=True, stop=True).then_inc(s.cs_mm, 1)
                e.wait_ge(s.cb_ok, h + 1)
                wait_alone(e, s.cs_sb, h + 1)
                for b in range(NB):
                    ins = e.transpose(pst[0:HEADS, b // 4, (b % 4) * P:(b % 4 + 1) * P], cs[:, b, :], ident[:, :])
                ins.then_inc(s.cs_tp, 1)
                edge(e, h, 3)

                def out_blocks(n, blocks):
                    for b in blocks:
                        if b == 0:
                            e.wait_ge(s.wo_lo, START + n + 1)
                            e.wait_ge(s.glo, 2 * n + 1)
                        if b == 4:
                            e.wait_ge(s.glo, 2 * n + 2)
                        if b >= 2:
                            e.wait_ge(s.oacc, START + NB * n + b - 1)
                        t = slice(b * P, (b + 1) * P)
                        mm3(e, pso[:, b % 2, :], g_hi[:, t], g_lo[:, t], w_hi[:, O, :], w_lo[:, O, :], True, True) \
                            .then_inc(s.op, 1)

                def pair(i, first, last):
                    n = h * PAIRS + i
                    e.wait_ge(s.wz_lo, START + n + 1)
                    for q in range(2):
                        e.wait_ge(s.xev, 2 * (h * TILES + i + 2) + q + 1)
                        project(psx[:, q, :], Z, q, s.zp)
                    if not first:
                        e.wait_ge(s.oacc, START + NB * (n - 1))
                        out_blocks(n - 1, range(0, 4))
                    e.wait_ge(s.xs, START + h * TILES + i + 3)
                    e.wait_ge(s.sin, START + n)
                    for b in range(NB):
                        ins = e.transpose(pst_b[:, b, :], xs[:, b * P:(b + 1) * P], ident[:, :])
                    ins.then_inc(s.xT, 1)
                    if not first:
                        out_blocks(n - 1, range(4, 8))
                    e.wait_ge(s.xd_r, n + 1)
                    for b in range(NB):
                        ins = e.matmul(pst_b[:, b, :], b_tok[:, b, :], xd[:, b, :], start=True, stop=True)
                    ins.then_inc(s.st, 1)
                    for q in range(2):
                        if q == 0:
                            e.wait_ge(s.mt_r, 2 * n + 2)
                            e.wait_ge(s.sin, START + n + 1)
                        e.wait_ge(s.y_read, START + 2 * n + q)
                        for b in range(4 * q, 4 * q + 4):
                            c = slice((b % 4) * P, (b % 4 + 1) * P)
                            for r in range(2):
                                hp = slice(r * HEAD_P, (r + 1) * HEAD_P)
                                e.matmul(psy[hp, 0, c], xdt[:, b, hp], mt[:, r, b * P:(b + 1) * P],
                                         start=True, stop=True)
                            ins = e.matmul(psy[:, 1, c], s_in[:, b, :], c_t[:, b * P:(b + 1) * P],
                                           start=True, stop=True)
                        ins.then_inc(s.yp, 1)
                        if not last:
                            if q == 0:
                                e.wait_ge(s.szr, START + n + 1)
                            project_x(i + 3, q)

                pair(0, True, False)
                with e.Fori(1, PAIRS - 1) as i:
                    pair(i, False, False)
                pair(PAIRS - 1, False, True)
                n = h * PAIRS + PAIRS - 1
                e.wait_ge(s.oacc, START + NB * n)
                out_blocks(n, range(NB))
                e.wait_ge(s.ssq, START + 2 * n + 2)
                for b in range(NB):
                    ins = e.matmul(psy[:, 0, b:b + 1], sumsq[:, b * P:(b + 1) * P], ones[:, 0:1],
                                   start=True, stop=True)
                ins.then_inc(s.ss_mm, 1)
                edge(e, h, 4)
                transpose_norm(1)
                edge(e, h, 5)

                def down(n):
                    for b in range(NB):
                        if b == 0:
                            e.wait_ge(s.hdlo, START + n + 1)
                            e.wait_ge(s.wd_lo, n + 1)
                            e.wait_ge(s.facc, START + NB * n)
                        if b >= 2:
                            e.wait_ge(s.facc, START + NB * n + b - 1)
                        t = slice(b * P, (b + 1) * P)
                        mm3(e, pso[:, b % 2, :], g_hi[:, t], g_lo[:, t], w_hi[:, O, :], w_lo[:, O, :], True, True) \
                            .then_inc(s.fp, 1)

                def up_gate(t):
                    n = h * FT + t
                    e.wait_ge(s.wg_lo, n + 1)
                    e.wait_ge(s.gh, START + n)
                    project(psx[:, 0, :], Z, 0, None)
                    project(psx[:, 1, :], Z, 1, s.gp)
                    e.wait_ge(s.wu_lo, n + 1)
                    e.wait_ge(s.hd, START + n)
                    project(pst[:, 0, :], X, 0, None)
                    project(pst[:, 1, :], X, 1, s.up)

                up_gate(0)
                with e.Fori(1, FT) as t:
                    up_gate(t)
                    down(h * FT + t - 1)
                down(h * FT + FT - 1)

        @block.vector
        def _(e):
            start_counters(e, s.y_read, s.taps, s.xs, s.szr, s.hd, s.sin, s.oacc, s.facc)
            st = Steps(e, s.dve_step)
            flat = lambda t: t[:, :, :].rearrange("p b k -> p (b k)")
            e.memset(ones[:, :], 1.0).then_inc(s.const_ok, 1)
            e.memset(halo[:, :, :], 0.0)
            e.memset(carry[:, :, :], 0.0)
            e.wait_ge(s.const_in, 16 * 12)
            e.wait_ge(s.mod_c, 3)
            e.scalar_tensor_tensor(out=c_silu[:, :], in0=c_tanh[:, :], scalar=1.0, in1=c_half[:, :],
                                   op0=ALU.add, op1=ALU.mult).then_inc(s.mod_s, 1)
            e.wait_ge(s.mod_s, 1)
            for k in range(KT):
                ins = e.tensor_copy(xdt[:, k, :], c_silu[:, k:k + 1].broadcast_to([P, P]))
            ins.then_inc(s.mod_sb, 1)
            e.tensor_scalar(flat(conv_w), flat(conv_w), 0.5, None, ALU.mult)
            e.tensor_scalar(conv_b[:, :], conv_b[:, :], 0.5, None, ALU.mult)
            e.tensor_scalar(ffn_gs[:, :], ffn_gs[:, :], 0.5, None, ALU.mult)
            e.wait_ge(s.wdt_hi, 1)
            e.tensor_tensor(wdt_lo[:, :, :], wdt_raw[:, :, :], wdt_hi[:, :, :].bitcast(F32), ALU.subtract) \
                .then_inc(s.wdt_lo, 1)
            e.wait_ge(s.wm_used, 6)
            st.mark(e.tensor_copy(mod_col[:, :, :].rearrange("p m k -> p (m k)"), psy[:, 0, 0:4 * KT]))
            for k, row in enumerate((gate_a, gate_b)):
                st.mark(e.tensor_copy(row[:, :], pso[:, k, :]))
                st.sync()
                st.link(e.tensor_scalar(xs[:, 0:HID], row[:, :], 0.0, 2.0, ALU.is_ge, ALU.mult))
                st.link(e.scalar_tensor_tensor(out=xs[:, 512:512 + HID], in0=row[:, :], scalar=-1.0, in1=row[:, :],
                                               op0=ALU.mult, op1=ALU.max))
                st.link(e.tensor_scalar(xs[:, 512:512 + HID], xs[:, 512:512 + HID], 0.25, None, ALU.max))
                st.link(e.scalar_tensor_tensor(out=row[:, :], in0=xs[:, 0:HID], scalar=-1.0,
                                               in1=xs[:, 512:512 + HID], op0=ALU.add, op1=ALU.mult))
            st.link(e.tensor_tensor(gate_b[:, :], gate_b[:, :], g[:, 0:HID], ALU.mult))
            for m in (1, 3):
                st.link(e.tensor_scalar(mod_col[:, m, :], mod_col[:, m, :], 1.0, None, ALU.add))
            assert st.count == DVE_STEPS["setup"], ("setup", st.count)

            with e.Fori(0, HALVES) as h:
                st.base, st.count = h * DVE_STEPS["half"] + DVE_STEPS["setup"], 0
                done = [0]

                def reciprocal_root(k):
                    e.wait_ge(s.root_r, 3 * h + k + 1)
                    st.link(e.reciprocal(rstd[:, :], root[:, :]))
                    st.link(e.tensor_tensor(root[:, :], rstd[:, :], rstd[:, :], ALU.mult))
                    st.link(e.tensor_tensor(root[:, :], root[:, :], var[:, :], ALU.mult))
                    st.link(e.tensor_scalar(root[:, :], root[:, :], -0.5, 1.5, ALU.mult, ALU.add))
                    st.link(e.tensor_tensor(rstd[:, :], rstd[:, :], root[:, :], ALU.mult))

                def layer_norm(which, k):
                    if which == 0:
                        e.wait_ge(s.x_in, 16 * (h + 1))
                    for b in range(NB):
                        st.mark(e.bn_stats(stat[:, b, :], acc[:, b, :]))
                    wait_alone(e, st.sem, st.base + st.count)
                    for b in range(NB):
                        st.mark(e.bn_aggr(mv[:, b, :], stat[:, b, :]))
                    st.sync()
                    e.tensor_scalar(var[:, :], mv[:, :, 1:2].rearrange("p b a -> p (b a)"), LN_EPS, None, ALU.add) \
                        .then_inc(s.var_r, 1)
                    reciprocal_root(k)
                    for b in range(NB):
                        n = (2 * h + which) * NB + b
                        if b >= 2:
                            e.wait_ge(s.tp, n - 1)
                        e.tensor_scalar(xn[:, b % 2, :], acc[:, b, :], mv[:, b, 0:1], rstd[:, b:b + 1],
                                        ALU.subtract, ALU.mult).then_inc(s.xn, 1)
                        if b >= 1:
                            split_h(which, b - 1)
                    split_h(which, NB - 1)

                def split_h(which, b):
                    u, n = b % 2, (2 * h + which) * NB + b
                    e.wait_ge(s.h32, n + 1)
                    t = slice(b * P, (b + 1) * P)
                    st.link(e.tensor_copy(ht_hi[:, :, t], h32[:, u]))
                    e.tensor_tensor(ht_lo[:, :, t], h32[:, u], ht_hi[:, :, t].bitcast(F32), ALU.subtract) \
                        .then_inc(s.ht, 1)

                edge(e, h, 1)
                layer_norm(0, 0)
                edge(e, h, 2)

                def convolve(j, dst):
                    m = h * TILES + j
                    e.wait_ge(s.tap0, m + 1)
                    for k in range(TAPS - 1):
                        ins = e.scalar_tensor_tensor(
                            out=conv[:, :], in0=xraw[:, k:k + TH],
                            scalar=conv_w[:, bass.ds(j, 1), k:k + 1].rearrange("p a k -> p (a k)"),
                            in1=conv[:, :], op0=ALU.mult, op1=ALU.add)
                        if k < TAPS - 2:
                            st.link(ins)
                        else:
                            ins.then_inc(s.taps, 1)
                    e.wait_ge(s.thc, m + 1)
                    e.scalar_tensor_tensor(out=dst, in0=conv_th[:, :], scalar=1.0, in1=conv[:, :],
                                           op0=ALU.add, op1=ALU.mult).then_inc(s.xs, 1)

                convolve(0, b_t[:, :])
                convolve(1, c_t[:, :])
                e.wait_ge(s.btok_tp, h + 1)
                e.tensor_copy(b_tok[:, :, :], pst_b[:, :, :]).then_inc(s.btok, 1)
                e.wait_ge(s.cb_mm, h + 1)
                e.tensor_tensor(cb[:, :, :], pst_b[:, :, :], tri[:, :].unsqueeze(1).broadcast_to([P, NB, P]),
                                ALU.mult).then_inc(s.cb_ok, 1)
                v, ab, ee, uu, lg = (sq[:, 0:512], conv_th[:, 0:512], conv_th[:, 512:1024], z_th[:, 0:512],
                                     z_th[:, 512:1024])
                d, zero = g[:, 0:512], g[:, 512:1024]
                e.wait_ge(s.dt_mm, h + 1)
                st.link(e.tensor_tensor(v.rearrange("p (b k) -> p b k", b=NB),
                                        psy[:, 0, :].rearrange("p (b k) -> p b k", b=NB),
                                        dt_bias[:, :].unsqueeze(1).broadcast_to([P, NB, HEADS]), ALU.add))
                e.scalar_tensor_tensor(out=ab, in0=v, scalar=-1.0, in1=v, op0=ALU.mult, op1=ALU.max) \
                    .then_inc(s.dt_abs, 1)
                e.wait_ge(s.dt_exp, h + 1)
                e.tensor_scalar(uu, ee, 1.0, None, ALU.add).then_inc(s.dt_u, 1)
                e.wait_ge(s.dt_u, h + 1)
                st.link(e.tensor_scalar(d, uu, -1.0, None, ALU.add))
                st.link(e.tensor_scalar(zero, d, 0.0, None, ALU.is_equal))
                st.link(e.tensor_tensor(d, d, zero, ALU.add))
                st.link(e.reciprocal(d, d))
                st.link(e.tensor_tensor(d, d, ee, ALU.mult))
                e.wait_ge(s.dt_ln, h + 1)
                st.link(e.tensor_tensor(d, d, lg, ALU.mult))
                st.link(e.tensor_tensor(zero, zero, ee, ALU.mult))
                st.link(e.tensor_tensor(d, d, zero, ALU.add))
                st.link(e.scalar_tensor_tensor(out=d, in0=v, scalar=0.0, in1=d, op0=ALU.max, op1=ALU.add))
                st.link(e.tensor_scalar(flat(dt), d, 0.0, DT_MAX, ALU.max, ALU.min))
                e.scalar_tensor_tensor(out=dt_end[:, :, :], in0=dt[:, :, :], scalar=-1.0,
                                       in1=exp_a[:, :].unsqueeze(1).broadcast_to([P, NB, HEADS]),
                                       op0=ALU.mult, op1=ALU.mult).then_inc(s.dta, 1)
                e.wait_ge(s.cs_mm, h + 1)
                e.tensor_copy(flat(cs), psy[:, 0, :]).then_inc(s.cs_sb, 1)
                e.wait_ge(s.cs_sb, h + 1)
                st.link(e.tensor_tensor(flat(dt_end), psy[:, 1, :], flat(cs), ALU.subtract))
                e.tensor_scalar(flat(dt_end), flat(dt_end), 0.0, None, ALU.min).then_inc(s.csm, 1)
                e.wait_ge(s.dec, 2 * h + 2)
                e.tensor_tensor(flat(dt_end), flat(dt_end), flat(dt), ALU.mult)
                edge(e, h, 3)

                def accumulate(n, blocks, fresh, src_done, dst, done):
                    for b in blocks:
                        e.wait_ge(src_done, START + NB * n + b + 1)
                        if fresh:
                            ins = e.tensor_copy(dst[:, b, :], pso[:, b % 2, :])
                        else:
                            ins = e.tensor_tensor(dst[:, b, :], pso[:, b % 2, :], dst[:, b, :], ALU.add)
                        ins.then_inc(done, 1)

                def heads(table, i, blocks=NB):
                    return table[:, :, bass.ds(2 * i, 2)].unsqueeze(3).broadcast_to([P, NB, 2, HEAD_P])

                def pair(i, first, fresh):
                    n = h * PAIRS + i
                    convolve(i + 2, xs[:, :])
                    e.wait_ge(s.seg, START + 2 * n + 2)
                    e.tensor_scalar(mt, mt, 0.0, None, ALU.min).then_inc(s.seg_min, 1)
                    e.wait_ge(s.thz, n + 1)
                    e.scalar_tensor_tensor(out=sz[:, :], in0=z_th[:, :], scalar=1.0,
                                           in1=psx[:, :, :].rearrange("p a n -> p (a n)"),
                                           op0=ALU.add, op1=ALU.mult).then_inc(s.szr, 1)
                    if not first:
                        accumulate(n - 1, range(0, 4), fresh, s.op, acc, s.oacc)
                    e.wait_ge(s.xT, n + 1)
                    four = "p b (r q) -> p b r q"
                    e.tensor_tensor(xdt[:, :, :].rearrange(four, r=2), pst_b[:, :, :].rearrange(four, r=2),
                                    heads(dt, i), ALU.mult).then_inc(s.xdt_r, 1)
                    e.tensor_tensor(xd[:, :, :].rearrange(four, r=2), pst_b[:, :, :].rearrange(four, r=2),
                                    heads(dt_end, i), ALU.mult).then_inc(s.xd_r, 1)
                    for r in range(2):
                        e.wait_ge(s.ex, 2 * n + r + 1)
                        e.tensor_tensor(mt[:, r, :], mt[:, r, :], cb[:, :, :].rearrange("p b t -> p (b t)"),
                                        ALU.mult).then_inc(s.mt_r, 1)
                    if not first:
                        accumulate(n - 1, range(4, 8), fresh, s.op, acc, s.oacc)
                    st.link(e.tensor_copy(s_in[:, 0, :], carry[:, bass.ds(i, 1), :].rearrange("p a n -> p (a n)")))
                    e.wait_ge(s.st, n + 1)
                    for b in range(NB):
                        for r in range(2):
                            hp = slice(r * HEAD_P, (r + 1) * HEAD_P)
                            dst = s_in[:, b + 1, hp] if b < NB - 1 else \
                                carry[:, bass.ds(i, 1), hp].rearrange("p a n -> p (a n)")
                            ins = e.scalar_tensor_tensor(out=dst, in0=s_in[:, b, hp],
                                                         scalar=e_last[:, b, bass.ds(2 * i + r, 1)],
                                                         in1=pst_b[:, b, hp], op0=ALU.mult, op1=ALU.add)
                            if b < NB - 1:
                                st.mark(ins)
                        if b < NB - 1:
                            st.sync()
                    ins.then_inc(s.sin, 1)
                    for q in range(2):
                        c = slice(q * 512, q * 512 + 512)
                        e.wait_ge(s.yp, START + 2 * n + q + 1)
                        e.wait_ge(s.erow_in, 32 * (n + 1))
                        st.link(e.tensor_tensor(g[:, c], psy[:, 1, :], e_row[:, c], ALU.mult))
                        st.link(e.scalar_tensor_tensor(out=g[:, c], in0=xs[:, c], scalar=d_col[:, bass.ds(i, 1)],
                                                       in1=g[:, c], op0=ALU.mult, op1=ALU.add))
                        ins = e.tensor_tensor(g[:, c], psy[:, 0, :], g[:, c], ALU.add)
                        ins.then_inc(s.y_read, 1)
                        e.wait_ge(s.y_read, START + 2 * n + q + 1)
                        e.tensor_tensor(g[:, c], g[:, c], sz[:, c], ALU.mult).then_inc(s.g_r, 1)

                pair(0, True, False)
                pair(1, False, True)
                at, base = st.count, st.base
                with e.Fori(2, PAIRS) as i:
                    st.base, st.count = base + (i - 2) * DVE_STEPS["pair"] + at, 0
                    pair(i, False, False)
                    assert st.count == DVE_STEPS["pair"], ("pair", st.count)
                st.base, st.count = base, at + (PAIRS - 2) * DVE_STEPS["pair"]
                n = h * PAIRS + PAIRS - 1
                accumulate(n, range(NB), False, s.op, acc, s.oacc)
                e.wait_ge(s.ss_mm, h + 1)
                e.tensor_scalar(var[:, :], psy[:, 0, 0:NB], 1.0 / (4 * INTER), RMS_EPS, ALU.mult, ALU.add) \
                    .then_inc(s.var_r, 1)
                edge(e, h, 4)
                reciprocal_root(1)
                st.link(e.tensor_scalar(rstd[:, :], rstd[:, :], 0.5, None, ALU.mult))
                for b in range(NB):
                    st.link(e.scalar_tensor_tensor(out=acc[:, b, :], in0=acc[:, b, :], scalar=rstd[:, b:b + 1],
                                                   in1=gate_a[:, :], op0=ALU.mult, op1=ALU.mult))
                    e.wait_ge(s.xres_in[b % 2], 16 * (h * NB // 2 + b // 2 + 1))
                    e.tensor_tensor(acc[:, b, :], acc[:, b, :], sq[:, (b % 2) * HID:(b % 2 + 1) * HID], ALU.add) \
                        .then_inc(s.x2, 1)
                e.wait_ge(s.x2, h * NB + NB)
                layer_norm(1, 2)
                edge(e, h, 5)

                def ffn(t, first, fresh):
                    n = h * FT + t
                    e.wait_ge(s.thg, n + 1)
                    st.link(e.scalar_tensor_tensor(out=conv_th[:, :], in0=conv_th[:, :], scalar=1.0, in1=conv[:, :],
                                                   op0=ALU.add, op1=ALU.mult))
                    e.wait_ge(s.up, START + n + 1)
                    e.wait_ge(s.hdlo, START + n)
                    e.scalar_tensor_tensor(out=g[:, :], in0=pst[:, :, :].rearrange("p a n -> p (a n)"),
                                           scalar=ffn_us[:, bass.ds(t, 1)], in1=conv_th[:, :],
                                           op0=ALU.mult, op1=ALU.mult).then_inc(s.hd, 1)
                    if not first:
                        accumulate(n - 1, range(NB), fresh, s.fp, f_acc, s.facc)

                ffn(0, True, False)
                ffn(1, False, True)
                at, base = st.count, st.base
                with e.Fori(2, FT) as t:
                    st.base, st.count = base + (t - 2) * DVE_STEPS["ffn"] + at, 0
                    ffn(t, False, False)
                    assert st.count == DVE_STEPS["ffn"], ("ffn", st.count)
                st.base, st.count = base, at + (FT - 2) * DVE_STEPS["ffn"]
                n = h * FT + FT - 1
                for b in range(NB):
                    accumulate(n, [b], False, s.fp, f_acc, s.facc)
                    e.wait_ge(s.facc, START + NB * n + b + 1)
                    st.link(e.tensor_tensor(f_acc[:, b, :], f_acc[:, b, :], gate_b[:, :], ALU.mult))
                    e.tensor_tensor(acc[:, b, :], acc[:, b, :], f_acc[:, b, :], ALU.add).then_inc(s.fin, 1)
                assert st.count == DVE_STEPS["half"], ("half", st.count)

        @block.gpsimd
        def _(e):
            start_counters(e, s.wx_lo, s.wz_lo, s.wo_lo, s.seg, s.ssq, s.hdlo)
            e.memset(ident[:, :], 0.0).then_inc(s.const_ok, 1)
            e.memset(tri[:, :], 1.0).then_inc(s.const_ok, 1)
            e.wait_ge(s.const_ok, 3)
            e.affine_select(out=ident[:, :], in_=ident[:, :], compare_op=ALU.not_equal, fill=1.0, base=0,
                            pattern=[[-1, P]], channel_multiplier=1).then_inc(s.const_ok, 1)
            e.affine_select(out=tri[:, :], in_=tri[:, :], compare_op=ALU.is_ge, fill=0.0, base=0,
                            pattern=[[1, P]], channel_multiplier=-1).then_inc(s.const_ok, 1)
            with e.Fori(0, HALVES) as h:
                edge(e, h, 1)
                edge(e, h, 2)

                def low(k, hi_done, count, done):
                    e.wait_ge(hi_done, count)
                    e.tensor_tensor(w_lo[:, k, :], w_raw[:, k, :], w_hi[:, k, :].bitcast(F32), ALU.subtract) \
                        .then_inc(done, 1)

                for j in range(3):
                    low(X, s.wx_hi, h * TILES + j + 1, s.wx_lo)
                low(Z, s.wz_hi, h * PAIRS + 1, s.wz_lo)
                e.memset(sumsq[:, :], 0.0)
                edge(e, h, 3)

                def blocks(row):
                    return row.rearrange("p (b t) -> p b t", b=NB)

                def cs_s(i, r):
                    return cs[:, :, bass.ds(2 * i + r, 1)].broadcast_to([P, NB, P])

                def pair(i, last):
                    n = h * PAIRS + i
                    for r in range(2):
                        e.wait_ge(s.csrow_in[r], 16 * (n + 1))
                        e.wait_ge(s.yp, START + 2 * n)
                        e.tensor_tensor(blocks(mt[:, r, :]), blocks(cs_row[:, r, :]), cs_s(i, r), ALU.subtract) \
                            .then_inc(s.seg, 1)
                    if not last:
                        low(X, s.wx_hi, h * TILES + i + 4, s.wx_lo)
                        low(Z, s.wz_hi, n + 2, s.wz_lo)
                    low(O, s.wo_hi, n + 1, s.wo_lo)
                    for q in range(2):
                        c = slice(q * 512, q * 512 + 512)
                        e.wait_ge(s.ghi, 2 * n + q + 1)
                        e.tensor_tensor(g_lo[:, c], g[:, c], g_hi[:, c].bitcast(F32), ALU.subtract) \
                            .then_inc(s.glo, 1)
                        e.wait_ge(s.sqr, 2 * n + q + 1)
                        e.tensor_tensor(sumsq[:, c], sumsq[:, c], sq[:, c], ALU.add).then_inc(s.ssq, 1)

                with e.Fori(0, PAIRS - 1) as i:
                    pair(i, False)
                pair(PAIRS - 1, True)
                edge(e, h, 4)
                edge(e, h, 5)
                with e.Fori(0, FT) as t:
                    n = h * FT + t
                    low(Z, s.wg_hi, n + 1, s.wg_lo)
                    low(X, s.wu_hi, n + 1, s.wu_lo)
                    low(O, s.wd_hi, n + 1, s.wd_lo)
                    e.wait_ge(s.hdhi, n + 1)
                    e.tensor_tensor(g_lo[:, :], g[:, :], g_hi[:, :].bitcast(F32), ALU.subtract).then_inc(s.hdlo, 1)


def tiles(w, n):
    return np.ascontiguousarray(w.reshape(KT, P, n, P).transpose(2, 1, 0, 3).reshape(n, P, KT * P))


def kernel(**inputs):
    import concourse.bacc as bacc
    from concourse.bass_utils import run_bass_kernel_spmd

    v = {k: np.asarray(x) for k, x in inputs.items()}
    w_in = v["L0_attn_W_in"]
    conv_dim = INTER + 2 * STATE
    w_z, w_xbc, w_dt = w_in[:, :INTER], w_in[:, INTER:INTER + conv_dim], w_in[:, INTER + conv_dim:]

    def bc_first(t):
        return np.concatenate([t[..., INTER:], t[..., :INTER]], axis=-1)

    def col(t, n):
        return np.ascontiguousarray(t.reshape(n, P).T)

    arrays = {
        "x": v["L0_attn_hidden_states"].reshape(TOKENS, HID),
        "wx": tiles(bc_first(w_xbc), TILES),
        "wz": tiles(w_z, PAIRS),
        "wdt": w_dt.reshape(KT, P, HEADS).transpose(1, 0, 2),
        "wo": v["L0_attn_W_out"].reshape(PAIRS, P, HID),
        "conv_w": bc_first(v["L0_attn_conv_w"]).reshape(TAPS, TILES, P).transpose(2, 1, 0),
        "conv_b": col(bc_first(v["L0_attn_conv_b"]), TILES),
        "dt_bias": v["L0_attn_dt_bias"], "a_log": v["L0_attn_A_log"],
        "d": v["L0_attn_D"].reshape(PAIRS, 2).T,
        "norm_w": col(v["L0_attn_norm_weight"], PAIRS),
        "wg": tiles(v["L0_ffn_gate_w"].T, FT), "wu": tiles(v["L0_ffn_up_w"].T, FT),
        "wd": v["L0_ffn_down_w"].T.reshape(FT, P, HID),
        "gate_s": col(v["L0_ffn_gate_s"], FT), "up_s": col(v["L0_ffn_up_s"], FT),
        "down_s": v["L0_ffn_down_s"],
        "c": col(v["L0_c"], KT), "wmod": v["L0_wmod"],
    }
    arrays = {f"in_{k}": np.ascontiguousarray(t) for k, t in arrays.items()}
    nc = bacc.Bacc("TRN2", target_bir_lowering=False, num_devices=1)
    aps = {k[3:]: nc.dram_tensor(k, t.shape, mybir.dt.from_np(t.dtype), kind="ExternalInput").ap()
           for k, t in arrays.items()}
    out = nc.dram_tensor("out", (TOKENS, HID), F32, kind="ExternalOutput").ap()
    build(nc, aps, out)
    r = run_bass_kernel_spmd(nc, [arrays], core_ids=[0])
    return np.asarray(r.results[0]["out"]).reshape(1, TOKENS, HID)
```

```python
from contextlib import ExitStack

import numpy as np

import concourse.bass as bass
from concourse import mybir

F32 = mybir.dt.float32
F32R = mybir.dt.float32r
ALU = mybir.AluOpType
ACT = mybir.ActivationFunctionType

P = 128
TOKENS, HID = 2048, 512
HEADS, HEAD_P, STATE = 64, 64, 128
INTER = HEADS * HEAD_P
KT = HID // P
HALVES = 2
TH = TOKENS // HALVES
NB = TH // P
BANKS = TH // 512
PAIRS = INTER // P
GROUPS = PAIRS // 2
TILES = PAIRS + 2
TAPS = 4
FFN = 1408
FT = FFN // P
LN_EPS = RMS_EPS = 1e-5
DT_MAX = 100.0
EDGES = 5
ENGINES = 5
START = 5

DVE_STEPS = dict(setup=14, half=647, pair=34, ffn=1)


class Steps:

    def __init__(self, engine, sem):
        self.engine, self.sem, self.base, self.count = engine, sem, 0, 0

    def mark(self, ins):
        ins.then_inc(self.sem, 1)
        self.count += 1

    def sync(self):
        self.engine.wait_ge(self.sem, self.base + self.count)

    def link(self, ins):
        self.mark(ins)
        self.sync()


class Semaphores:

    def __init__(self, sem):
        self.edge = sem("edge")
        self.passed = sem("passed")
        self.const_in = sem("const_in")
        self.const_ok = sem("const_ok")
        self.dve_step = sem("dve_step")
        self.wm_in = sem("wm_in")
        self.wm_used = sem("wm_used")
        self.mod_c = sem("mod_c")
        self.mod_s = sem("mod_s")
        self.mod_sb = sem("mod_sb")
        self.x_in = sem("x_in")
        self.xn = sem("xn")
        self.tp = sem("tp")
        self.h32 = sem("h32")
        self.ht = sem("ht")
        self.wdt_hi = sem("wdt_hi")
        self.wdt_lo = sem("wdt_lo")
        self.dt_mm = sem("dt_mm")
        self.dt_abs = sem("dt_abs")
        self.dt_exp = sem("dt_exp")
        self.dt_u = sem("dt_u")
        self.dt_ln = sem("dt_ln")
        self.dta = sem("dta")
        self.cs_mm = sem("cs_mm")
        self.cs_sb = sem("cs_sb")
        self.csm = sem("csm")
        self.dec = sem("dec")
        self.cs_tp = sem("cs_tp")
        self.cs_row_ok = sem("cs_row_ok")
        self.scratch = sem("scratch")
        self.cb_mm = sem("cb_mm")
        self.cb_ok = sem("cb_ok")
        self.btok_tp = sem("btok_tp")
        self.btok = sem("btok")
        self.wx_in = sem("wx_in")
        self.wx_hi = sem("wx_hi")
        self.wx_lo = sem("wx_lo")
        self.wz_in = sem("wz_in")
        self.wz_hi = sem("wz_hi")
        self.wz_lo = sem("wz_lo")
        self.wo_in = sem("wo_in")
        self.wo_wn = sem("wo_wn")
        self.wo_hi = sem("wo_hi")
        self.wo_lo = sem("wo_lo")
        self.xp = sem("xp")
        self.halo_in = sem("halo_in")
        self.xev = sem("xev")
        self.tap0 = sem("tap0")
        self.tap_k = sem("tap_k")
        self.taps = sem("taps")
        self.thc = sem("thc")
        self.xs = sem("xs")
        self.zp = sem("zp")
        self.thz = sem("thz")
        self.szr = sem("szr")
        self.xT = sem("xT")
        self.xdt_r = sem("xdt_r")
        self.xd_r = sem("xd_r")
        self.st = sem("st")
        self.sin = sem("sin")
        self.erow_in = sem("erow_in")
        self.seg = sem("seg")
        self.relu = sem("relu")
        self.ex = sem("ex")
        self.mt_r = sem("mt_r")
        self.yp = sem("yp")
        self.y_read = sem("y_read")
        self.x_skip = sem("x_skip")
        self.y_skip = sem("y_skip")
        self.g_r = sem("g_r")
        self.ghi = sem("ghi")
        self.glo = sem("glo")
        self.sqr = sem("sqr")
        self.ssq = sem("ssq")
        self.op = sem("op")
        self.oacc = sem("oacc")
        self.ss_mm = sem("ss_mm")
        self.x2 = sem("x2")
        self.var_r = sem("var_r")
        self.root_r = sem("root_r")
        self.wg_in = sem("wg_in")
        self.wg_hi = sem("wg_hi")
        self.wg_lo = sem("wg_lo")
        self.wu_in = sem("wu_in")
        self.wu_hi = sem("wu_hi")
        self.wu_lo = sem("wu_lo")
        self.wd_in = sem("wd_in")
        self.wd_hi = sem("wd_hi")
        self.wd_lo = sem("wd_lo")
        self.gp = sem("gp")
        self.up = sem("up")
        self.gh = sem("gh")
        self.thg = sem("thg")
        self.hd = sem("hd")
        self.hdhi = sem("hdhi")
        self.hdlo = sem("hdlo")
        self.fp = sem("fp")
        self.facc = sem("facc")
        self.fin = sem("fin")
        self.out_ok = sem("out_ok")
        self.xres_in = [sem(f"xres_in{k}") for k in range(2)]
        self.csrow_in = [sem(f"csrow_in{k}") for k in range(2)]


def build(nc, a, out):
    ctx = ExitStack()
    with ctx:
        def sb(name, shape, dt=F32):
            return ctx.enter_context(nc.sbuf_tensor(name, shape, dt))

        def ps(name, shape):
            return ctx.enter_context(nc.psum_tensor(name, shape, F32))

        def sem(name):
            return ctx.enter_context(nc.semaphore(name))

        ident = sb("ident", [P, P])
        tri = sb("tri", [P, P])
        ones = sb("ones", [P, P])
        c_col = sb("c_col", [P, KT])
        c_half = sb("c_half", [P, KT])
        c_tanh = sb("c_tanh", [P, KT])
        c_silu = sb("c_silu", [P, KT])
        mod_col = sb("mod_col", [P, 4, KT])
        gate_a = sb("gate_a", [P, HID])
        gate_b = sb("gate_b", [P, HID])
        conv_w = sb("conv_w", [P, TILES, TAPS])
        conv_b = sb("conv_b", [P, TILES])
        d_col = sb("d_col", [P, PAIRS])
        norm_col = sb("norm_col", [P, PAIRS])
        ffn_gs = sb("ffn_gs", [P, FT])
        ffn_us = sb("ffn_us", [P, FT])
        dt_bias = sb("dt_bias", [P, HEADS])
        exp_a = sb("exp_a", [P, HEADS])
        ht_hi = sb("ht_hi", [P, KT, TH], F32R)
        ht_lo = sb("ht_lo", [P, KT, TH], F32R)
        acc = sb("acc", [P, NB, HID])
        c_t = sb("c_t", [P, TH])
        b_tok = sb("b_tok", [P, NB, STATE])
        cb = sb("cb", [P, NB, P])
        dt = sb("dt", [P, NB, HEADS])
        cs = sb("cs", [P, NB, HEADS])
        dt_end = sb("dt_end", [P, NB, HEADS])
        e_last = sb("e_last", [P, NB, HEADS])
        halo = sb("halo", [P, TILES, TAPS - 1])
        carry = sb("carry", [P, PAIRS, P])
        sumsq = sb("sumsq", [P, TH])
        big = sb("big", [P, 4, TH])
        cs_row, mt = big[:, 0:2, :], big[:, 2:4, :]
        e_row = sb("e_row", [P, TH])
        xraw = sb("xraw", [P, TAPS - 1 + TH])
        conv = sb("conv", [P, TH])
        conv_th = sb("conv_th", [P, TH])
        xs = sb("xs", [P, TH])
        z_th = sb("z_th", [P, TH])
        sz = sb("sz", [P, TH])
        xdt = sb("xdt", [P, NB, P])
        xd = sb("xd", [P, NB, P])
        s_in = sb("s_in", [P, NB, P])
        g = sb("g", [P, TH])
        x_skip = sb("x_skip", [P, TH])
        g_hi = sb("g_hi", [P, 2, TH], F32R)
        g_lo = sb("g_lo", [P, 2, TH], F32R)
        X, Z, O = 0, 1, 2
        w_raw = sb("w_raw", [P, 3, 512])
        w_hi = sb("w_hi", [P, 4, 512], F32R)
        w_lo = sb("w_lo", [P, 4, 512], F32R)
        wdt_raw = g[:, 512:512 + KT * HEADS].rearrange("p (k m) -> p k m", k=KT)
        wdt_hi = sb("wdt_hi", [P, KT, HEADS], F32R)
        wdt_lo = sb("wdt_lo", [P, KT, HEADS], F32R)
        stat = sb("stat", [P, NB, 6])
        mv = sb("mv", [P, NB, 2])
        var = sb("var", [P, NB])
        root = sb("root", [P, NB])
        rstd = sb("rstd", [P, NB])
        xn = conv_th[:, :].rearrange("p (u n) -> p u n", u=2)
        h32 = z_th[:, :].rearrange("p (u k t) -> p u k t", u=2, k=KT)
        b_t = sz
        cs_t, ecs_t = xdt[0:HEADS], xd[0:HEADS]
        f_acc = big[:, :, :].rearrange("p a (b n) -> p (a b) n", n=HID)
        wmod_sb = big[:, 0:2, :].rearrange("p a (b n) -> p (a b) n", n=HID)

        psx = ps("psx", [P, BANKS, 512])
        pst = ps("pst", [P, BANKS, 512])
        psy = ps("psy", [P, 2, 512])
        pso = ps("pso", [P, 2, 512])
        pst_b = pst[:, :, :].rearrange("p a (b n) -> p (a b) n", n=P)

        s = Semaphores(sem)

        scr_cs = nc.dram_tensor("scr_cs", (HALVES, HEADS, TH), F32).ap()
        scr_ecs = nc.dram_tensor("scr_ecs", (HALVES, HEADS, TH), F32).ap()
        x_v = a["x"].rearrange("(h b p) n -> h b p n", h=HALVES, p=P)
        out_v = out.rearrange("(h b p) n -> h b p n", h=HALVES, p=P)
        wmod_v = a["wmod"].rearrange("(k p) (m n) -> m p k n", p=P, n=HID)

        def wait_alone(e, which, value):
            e.wait_ge(which, value)
            e.sem_inc(s.passed, 1)

        def start_counters(e, *counters):
            for counter in counters:
                e.sem_inc(counter, START)

        def edge(e, h, k):
            e.drain().then_inc(s.edge, 1)
            wait_alone(e, s.edge, (h * EDGES + k) * ENGINES)

        def mm3(e, dst, w_h, w_l, m_h, m_l, start, stop):
            e.matmul(dst, w_h, m_h, start=start, stop=False)
            e.matmul(dst, w_h, m_l, start=False, stop=False)
            return e.matmul(dst, w_l, m_h, start=False, stop=stop)

        block = ctx.enter_context(nc.Block())

        @block.sync
        def _(e):
            consts = [
                (c_col[:, :], a["c"]), (conv_w[:, :, :], a["conv_w"]), (conv_b[:, :], a["conv_b"]),
                (norm_col[:, :], a["norm_w"]), (ffn_gs[:, :], a["gate_s"]), (ffn_us[:, :], a["up_s"]),
                (wdt_raw, a["wdt"]),
                (dt_bias[:, :], a["dt_bias"].partition_broadcast(P)),
                (exp_a[:, :], a["a_log"].partition_broadcast(P)),
                (d_col[0:HEAD_P, :], a["d"][0].partition_broadcast(HEAD_P)),
                (d_col[HEAD_P:P, :], a["d"][1].partition_broadcast(HEAD_P)),
                (g[:, 0:HID], a["down_s"].partition_broadcast(P)),
            ]
            for dst, src in consts:
                e.dma_start(dst, src).then_inc(s.const_in, 16)
            for m in range(6):
                if m:
                    e.wait_ge(s.wm_used, m)
                e.dma_start(wmod_sb, wmod_v[m]).then_inc(s.wm_in, 16)
            with e.Fori(0, HALVES) as h:
                edge(e, h, 1)
                e.dma_start(acc[:, :, :], x_v[h].rearrange("b p n -> p b n")).then_inc(s.x_in, 16)
                e.dma_start(w_raw[:, X, :], a["wx"][0]).then_inc(s.wx_in, 16)
                edge(e, h, 2)
                e.dma_start(w_raw[:, Z, :], a["wz"][0]).then_inc(s.wz_in, 16)

                def load_x(j):
                    e.wait_ge(s.wx_lo, START + h * TILES + j)
                    e.dma_start(w_raw[:, X, :], a["wx"][j]).then_inc(s.wx_in, 16)

                def load_z(i):
                    e.wait_ge(s.wz_lo, START + h * PAIRS + i)
                    e.dma_start(w_raw[:, Z, :], a["wz"][i]).then_inc(s.wz_in, 16)

                def load_o(i):
                    e.wait_ge(s.wo_lo, START + h * PAIRS + i)
                    e.dma_start(w_raw[:, O, :], a["wo"][i]).then_inc(s.wo_in, 16)

                def load_cs(i):
                    e.wait_ge(s.mt_r, START + 2 * (h * PAIRS + i))
                    for r in range(2):
                        e.dma_start(cs_row[:, r, :], scr_cs[h, 2 * i + r].partition_broadcast(P)) \
                            .then_inc(s.csrow_in[r], 16)

                def load_e(i):
                    e.wait_ge(s.y_read, START + 2 * (h * PAIRS + i))
                    for r in range(2):
                        e.dma_start(e_row[r * HEAD_P:(r + 1) * HEAD_P, :],
                                    scr_ecs[h, 2 * i + r].partition_broadcast(HEAD_P)) \
                            .then_inc(s.erow_in, 16)

                for j in range(1, 4):
                    load_x(j)
                e.wait_ge(s.cs_row_ok, 2 * (h + 1))
                e.dma_start(scr_cs[h], cs_t.rearrange("p b t -> p (b t)")).then_inc(s.scratch, 16)
                e.dma_start(scr_ecs[h], ecs_t.rearrange("p b t -> p (b t)")).then_inc(s.scratch, 16)
                e.wait_ge(s.scratch, 32 * (h + 1))
                load_cs(0)
                load_x(4)
                load_z(1)
                edge(e, h, 3)

                def loads(i, parity, projects=True, convolves=True):
                    load_e(i)
                    if projects and not (isinstance(i, int) and i + 5 >= TILES):
                        load_x(i + 5)
                    if parity == 0:
                        load_o(i)
                    if projects:
                        load_z(i + 2)
                    if convolves:
                        load_cs(i + 1)
                    if parity == 1:
                        load_o(i)

                with e.Fori(0, GROUPS - 2) as k:
                    loads(2 * k, 0)
                    loads(2 * k + 1, 1)
                loads(PAIRS - 4, 0)
                loads(PAIRS - 3, 1)
                loads(PAIRS - 2, 0, projects=False)
                loads(PAIRS - 1, 1, projects=False, convolves=False)
                edge(e, h, 4)
                for b in range(NB):
                    if b >= 2:
                        e.wait_ge(s.x2, h * NB + b - 1)
                    e.dma_start(x_skip[:, (b % 2) * HID:(b % 2 + 1) * HID], x_v[h, b]).then_inc(s.xres_in[b % 2], 16)
                n = h * FT
                for k, (src, done) in enumerate(((a["wu"], s.wu_in), (a["wg"], s.wg_in), (a["wd"], s.wd_in))):
                    e.dma_start(w_raw[:, k, :], src[0]).then_inc(done, 16)
                edge(e, h, 5)
                with e.Fori(0, FT - 1) as t:
                    for k, (src, used, done) in enumerate(((a["wu"], s.wu_lo, s.wu_in), (a["wg"], s.wg_lo, s.wg_in),
                                                           (a["wd"], s.wd_lo, s.wd_in))):
                        e.wait_ge(used, h * FT + t + 1)
                        e.dma_start(w_raw[:, k, :], src[t + 1]).then_inc(done, 16)
                for b in range(NB):
                    e.wait_ge(s.fin, h * NB + b + 1)
                    e.dma_start(out_v[h, b], acc[:, b, :]).then_inc(s.out_ok, 16)
                wait_alone(e, s.out_ok, 16 * NB * (h + 1))

        @block.scalar
        def _(e):
            start_counters(e, s.gh)
            def copy(o, i, **kw):
                return e.activation(o, i, ACT.Copy, **kw)

            e.wait_ge(s.const_in, 16 * 12)
            e.activation(c_half[:, :], c_col[:, :], ACT.Copy, scale=0.5).then_inc(s.mod_c, 1)
            e.activation(c_tanh[:, :], c_col[:, :], ACT.Tanh, scale=0.5).then_inc(s.mod_c, 1)
            e.activation(exp_a[:, :], exp_a[:, :], ACT.Exp).then_inc(s.mod_c, 1)
            copy(wdt_hi[:, :, :], wdt_raw).then_inc(s.wdt_hi, 1)
            with e.Fori(0, HALVES) as h:
                edge(e, h, 1)

                def square_root(k):
                    e.wait_ge(s.var_r, 3 * h + k + 1)
                    e.activation(root[:, :], var[:, :], ACT.Sqrt).then_inc(s.root_r, 1)

                def transposed_norm(which):
                    for b in range(NB):
                        n = (2 * h + which) * NB + b
                        e.wait_ge(s.tp, n + 1)
                        if b >= 2:
                            e.wait_ge(s.ht, n - 1)
                        for k in range(KT):
                            ins = e.activation(h32[:, b % 2, k, :], pst[:, b % 2, k * P:(k + 1) * P], ACT.Identity,
                                               scale=mod_col[:, 2 * which + 1, k:k + 1],
                                               bias=mod_col[:, 2 * which, k:k + 1])
                        ins.then_inc(s.h32, 1)

                square_root(0)
                transposed_norm(0)
                edge(e, h, 2)

                def split_x(j):
                    m = h * TILES + j
                    e.wait_ge(s.wx_in, 16 * (m + 1))
                    e.wait_ge(s.xp, START + 2 * m)
                    copy(w_hi[:, X, :], w_raw[:, X, :]).then_inc(s.wx_hi, 1)

                def split_z(i):
                    n = h * PAIRS + i
                    e.wait_ge(s.wz_in, 16 * (n + 1))
                    e.wait_ge(s.zp, START + 2 * n)
                    copy(w_hi[:, Z, :], w_raw[:, Z, :]).then_inc(s.wz_hi, 1)

                def split_o(i, parity):
                    n = h * PAIRS + i
                    e.wait_ge(s.wo_in, 16 * (n + 1))
                    e.activation(w_raw[:, O, :], w_raw[:, O, :], ACT.Copy,
                                 scale=norm_col[:, bass.ds(i, 1)]).then_inc(s.wo_wn, 1)
                    e.wait_ge(s.wo_wn, n + 1)
                    e.wait_ge(s.op, START + NB // 2 * (n - parity))
                    copy(w_hi[:, O + parity, :], w_raw[:, O, :]).then_inc(s.wo_hi, 1)

                def evacuate_x(j, q):
                    m = h * TILES + j
                    e.wait_ge(s.xp, START + 2 * m + q + 1)
                    if q == 0:
                        e.wait_ge(s.taps, START + m)
                        copy(xraw[:, 0:TAPS - 1], halo[:, bass.ds(j, 1), :].rearrange("p a k -> p (a k)")) \
                            .then_inc(s.halo_in, 1)
                    c0 = TAPS - 1 + q * 512
                    copy(xraw[:, c0:c0 + 512], psx[:, q, :]).then_inc(s.xev, 1)

                def tap_last(j):
                    m = h * TILES + j
                    e.wait_ge(s.xev, 2 * (m + 1))
                    e.wait_ge(s.halo_in, m + 1)
                    e.wait_ge(s.xs, START + m)
                    e.activation(conv[:, :], xraw[:, TAPS - 1:TAPS - 1 + TH], ACT.Identity,
                                 scale=conv_w[:, bass.ds(j, 1), TAPS - 1:TAPS].rearrange("p a k -> p (a k)"),
                                 bias=conv_b[:, bass.ds(j, 1)]).then_inc(s.tap0, 1)
                    copy(halo[:, bass.ds(j, 1), :].rearrange("p a k -> p (a k)"), xraw[:, TH:TH + TAPS - 1])

                def silu_tanh(j):
                    m = h * TILES + j
                    e.wait_ge(s.taps, START + m + 1)
                    e.activation(conv_th[:, :], conv[:, :], ACT.Tanh).then_inc(s.thc, 1)

                for j in range(3):
                    split_x(j)
                    for q in range(2):
                        evacuate_x(j, q)
                    tap_last(j)
                    silu_tanh(j)
                split_x(3)
                split_z(0)
                for q in range(2):
                    evacuate_x(3, q)
                e.wait_ge(s.dt_abs, h + 1)
                e.activation(conv_th[:, 512:1024], conv_th[:, 0:512], ACT.Exp, scale=-1.0).then_inc(s.dt_exp, 1)
                e.wait_ge(s.dt_u, h + 1)
                e.activation(z_th[:, 512:1024], z_th[:, 0:512], ACT.Ln).then_inc(s.dt_ln, 1)
                e.wait_ge(s.csm, h + 1)
                flat = lambda t: t[:, :, :].rearrange("p b k -> p (b k)")
                e.activation(flat(dt_end), flat(dt_end), ACT.Exp).then_inc(s.dec, 1)
                e.activation(flat(e_last), psy[:, 1, :], ACT.Exp).then_inc(s.dec, 1)
                e.wait_ge(s.cs_tp, h + 1)
                copy(cs_t.rearrange("p b t -> p (b t)"), pst[0:HEADS, :, :].rearrange("p a n -> p (a n)")) \
                    .then_inc(s.cs_row_ok, 1)
                e.activation(ecs_t.rearrange("p b t -> p (b t)"), pst[0:HEADS, :, :].rearrange("p a n -> p (a n)"),
                             ACT.Exp).then_inc(s.cs_row_ok, 1)
                edge(e, h, 3)

                def round_g(i, parity, q):
                    n = h * PAIRS + i
                    c = slice(q * 512, q * 512 + 512)
                    e.wait_ge(s.g_r, 2 * n + q + 1)
                    e.wait_ge(s.op, START + NB // 2 * (n - parity - 2 * (1 - q)) + 4 * (1 - q)
                              if not isinstance(i, int) or i >= 2 else START + NB // 2 * h * PAIRS)
                    copy(g_hi[:, parity, c], g[:, c]).then_inc(s.ghi, 1)

                def square_g(i, q):
                    n = h * PAIRS + i
                    c = slice(q * 512, q * 512 + 512)
                    e.wait_ge(s.glo, 2 * n + q + 1)
                    e.activation(g[:, c], g[:, c], ACT.Square).then_inc(s.sqr, 1)

                def pair(i, parity, first=False, convolves=True, projects=True):
                    n = h * PAIRS + i
                    if convolves:
                        tap_last(i + 3)
                    if projects:
                        split_x(i + 4)
                    if parity == 0 and not first:
                        split_o(i - 1, 1)
                    for r in range(2):
                        e.wait_ge(s.seg, START + 2 * n + r + 1)
                        e.activation(cs_row[:, r, :], cs_row[:, r, :], ACT.Relu, scale=-1.0).then_inc(s.relu, 1)
                    if not first:
                        round_g(i - 1, 1 - parity, 0)
                    for r in range(2):
                        e.wait_ge(s.relu, 2 * n + r + 1)
                        e.activation(cs_row[:, r, :], cs_row[:, r, :], ACT.Exp, scale=-1.0).then_inc(s.ex, 1)
                    if not first and parity == 0:
                        round_g(i - 1, 1, 1)
                    e.wait_ge(s.zp, START + 2 * n + 2)
                    e.wait_ge(s.szr, START + n)
                    e.activation(z_th[:, :], psx[:, :, :].rearrange("p a n -> p (a n)"), ACT.Tanh, scale=0.5) \
                        .then_inc(s.thz, 1)
                    e.wait_ge(s.xs, START + h * TILES + i + 3)
                    e.wait_ge(s.y_skip, START + 2 * n)
                    e.activation(x_skip[:, :], xs[:, :], ACT.Copy, scale=d_col[:, bass.ds(i, 1)]) \
                        .then_inc(s.x_skip, 1)
                    if not first:
                        square_g(i - 1, 0)
                        if parity == 0:
                            square_g(i - 1, 1)
                    if convolves:
                        split_z(i + 1)
                        silu_tanh(i + 3)
                    if projects:
                        evacuate_x(i + 4, 0)
                    if parity == 1:
                        round_g(i - 1, 0, 1)
                        square_g(i - 1, 1)
                        split_o(i - 1, 0)
                    if projects:
                        evacuate_x(i + 4, 1)

                pair(0, 0, first=True)
                pair(1, 1)
                with e.Fori(1, GROUPS - 1) as k:
                    pair(2 * k, 0)
                    pair(2 * k + 1, 1)
                pair(PAIRS - 2, 0, projects=False)
                pair(PAIRS - 1, 1, convolves=False, projects=False)
                for q in range(2):
                    round_g(PAIRS - 1, 1, q)
                split_o(PAIRS - 1, 1)
                for q in range(2):
                    square_g(PAIRS - 1, q)
                edge(e, h, 4)
                square_root(1)
                square_root(2)
                transposed_norm(1)
                edge(e, h, 5)

                def ffn(t):
                    n = h * FT + t
                    def split(k, here, used, before, done):
                        e.wait_ge(here, 16 * (n + 1))
                        e.wait_ge(used, START + before)
                        copy(w_hi[:, k, :], w_raw[:, k, :]).then_inc(done, 1)

                    split(Z, s.wg_in, s.gp, n, s.wg_hi)
                    split(X, s.wu_in, s.up, n, s.wu_hi)
                    e.wait_ge(s.gp, START + n + 1)
                    e.wait_ge(s.hd, START + n)
                    e.activation(conv[:, :], psx[:, :, :].rearrange("p a n -> p (a n)"), ACT.Copy,
                                 scale=ffn_gs[:, bass.ds(t, 1)]).then_inc(s.gh, 1)
                    e.wait_ge(s.gh, START + n + 1)
                    e.activation(conv_th[:, :], conv[:, :], ACT.Tanh).then_inc(s.thg, 1)
                    split(O, s.wd_in, s.fp, NB * n, s.wd_hi)
                    e.wait_ge(s.hd, START + n + 1)
                    e.wait_ge(s.fp, START + NB * n)
                    copy(g_hi[:, 0, :], g[:, :]).then_inc(s.hdhi, 1)

                with e.Fori(0, FT) as t:
                    ffn(t)

        @block.tensor
        def _(e):
            start_counters(e, s.xp, s.zp, s.op, s.fp, s.yp, s.gp, s.up)
            e.wait_ge(s.const_ok, 5)
            e.wait_ge(s.mod_s, 1)
            for m in range(6):
                e.wait_ge(s.wm_in, 16 * (m + 1))
                if m in (2, 5):
                    e.wait_ge(s.mod_sb, 1)
                    for k in range(KT):
                        ins = e.matmul(pso[:, m // 3, :], xdt[:, k, :], wmod_sb[:, k, :],
                                       start=k == 0, stop=k == KT - 1)
                else:
                    for j in range(KT):
                        col = (m if m < 2 else m - 1) * KT + j
                        for k in range(KT):
                            ins = e.matmul(psy[:, 0, col:col + 1], wmod_sb[:, k, j * P:(j + 1) * P],
                                           c_silu[:, k:k + 1], start=k == 0, stop=k == KT - 1)
                ins.then_inc(s.wm_used, 1)
            with e.Fori(0, HALVES) as h:
                edge(e, h, 1)

                def transpose_norm(which):
                    for b in range(NB):
                        n = (2 * h + which) * NB + b
                        e.wait_ge(s.xn, n + 1)
                        if b >= 2:
                            e.wait_ge(s.h32, n - 1)
                        for k in range(KT):
                            ins = e.transpose(pst[:, b % 2, k * P:(k + 1) * P], xn[:, b % 2, k * P:(k + 1) * P],
                                              ident[:, :])
                        ins.then_inc(s.tp, 1)

                def project(dst, w, q, done):
                    for k in range(KT):
                        c, t = slice(k * P, (k + 1) * P), slice(q * 512, (q + 1) * 512)
                        ins = mm3(e, dst, w_hi[:, w, c], w_lo[:, w, c], ht_hi[:, k, t], ht_lo[:, k, t],
                                  k == 0, k == KT - 1)
                    if done is not None:
                        ins.then_inc(done, 1)
                    return ins

                def project_x(j, q):
                    if q == 0:
                        e.wait_ge(s.wx_lo, START + h * TILES + j + 1)
                    project(psx[:, q, :], X, q, s.xp)

                transpose_norm(0)
                edge(e, h, 2)
                for j in range(4):
                    for q in range(2):
                        if j:
                            e.wait_ge(s.xev, 2 * (h * TILES + j) + q - 1)
                        project_x(j, q)
                    if j == 0:
                        e.wait_ge(s.wdt_lo, 1)
                        for b in range(NB):
                            t = slice(b * P, (b + 1) * P)
                            for k in range(KT):
                                ins = mm3(e, psy[:, 0, b * HEADS:(b + 1) * HEADS], ht_hi[:, k, t], ht_lo[:, k, t],
                                          wdt_hi[:, k, :], wdt_lo[:, k, :], k == 0, k == KT - 1)
                        ins.then_inc(s.dt_mm, 1)
                e.wait_ge(s.xs, START + h * TILES + 1)
                for b in range(NB):
                    ins = e.transpose(pst_b[:, b, :], b_t[:, b * P:(b + 1) * P], ident[:, :])
                ins.then_inc(s.btok_tp, 1)
                e.wait_ge(s.xs, START + h * TILES + 2)
                e.wait_ge(s.btok, h + 1)
                for b in range(NB):
                    t = slice(b * P, (b + 1) * P)
                    ins = e.matmul(pst_b[:, b, :], b_t[:, t], c_t[:, t], start=True, stop=True)
                ins.then_inc(s.cb_mm, 1)
                e.wait_ge(s.dta, h + 1)
                flat = lambda t: t[:, :, :].rearrange("p b k -> p (b k)")
                e.matmul(psy[:, 0, :], tri[:, :], flat(dt_end), start=True, stop=True)
                e.matmul(psy[:, 1, :], ones[:, :], flat(dt_end), start=True, stop=True).then_inc(s.cs_mm, 1)
                e.wait_ge(s.cb_ok, h + 1)
                wait_alone(e, s.cs_sb, h + 1)
                for b in range(NB):
                    ins = e.transpose(pst[0:HEADS, b // 4, (b % 4) * P:(b % 4 + 1) * P], cs[:, b, :], ident[:, :])
                ins.then_inc(s.cs_tp, 1)
                edge(e, h, 3)

                def out_blocks(k, blocks):
                    n = h * GROUPS + k
                    for b in blocks:
                        if b % 4 == 0:
                            e.wait_ge(s.glo, 4 * n + 3 + b // 4)
                        if b == 0:
                            e.wait_ge(s.wo_lo, START + 2 * n + 2)
                        e.wait_ge(s.oacc, START + NB * n + b - 1 if b else START + NB * n)
                        t = slice(b * P, (b + 1) * P)
                        for parity in range(2):
                            ins = mm3(e, pso[:, b % 2, :], g_hi[:, parity, t], g_lo[:, parity, t],
                                      w_hi[:, O + parity, :], w_lo[:, O + parity, :], parity == 0, parity == 1)
                        ins.then_inc(s.op, 1)

                def transpose_x(i):
                    n = h * PAIRS + i
                    e.wait_ge(s.xs, START + h * TILES + i + 3)
                    e.wait_ge(s.sin, START + n)
                    for b in range(NB):
                        ins = e.transpose(pst_b[:, b, :], xs[:, b * P:(b + 1) * P], ident[:, :])
                    ins.then_inc(s.xT, 1)

                def project_z(i, q):
                    n = h * PAIRS + i
                    if q == 0:
                        e.wait_ge(s.wz_lo, START + n + 1)
                    if not isinstance(i, int) or i + 3 < TILES:
                        e.wait_ge(s.xev, 2 * (h * TILES + i + 3) + q + 1)
                    project(psx[:, q, :], Z, q, s.zp)

                def both_parts(i, q):
                    n = h * PAIRS + i
                    e.wait_ge(s.y_read, START + 2 * n + q)
                    for b in range(4 * q, 4 * q + 4):
                        c = slice((b % 4) * P, (b % 4 + 1) * P)
                        for r in range(2):
                            hp = slice(r * HEAD_P, (r + 1) * HEAD_P)
                            e.matmul(psy[hp, 0, c], xdt[:, b, hp], mt[:, r, b * P:(b + 1) * P],
                                     start=True, stop=True)
                        ins = e.matmul(psy[:, 1, c], s_in[:, b, :], c_t[:, b * P:(b + 1) * P],
                                       start=True, stop=True)
                    ins.then_inc(s.yp, 1)

                def pair(i, parity, group=None, projects=True, last=False):
                    n = h * PAIRS + i
                    blocks = range(4 * parity, 4 * parity + 4)
                    project_z(i, 0)
                    e.wait_ge(s.xd_r, n + 1)
                    e.wait_ge(s.xdt_r, n + 1)
                    for b in range(NB):
                        ins = e.matmul(pst_b[:, b, :], b_tok[:, b, :], xd[:, b, :], start=True, stop=True)
                    ins.then_inc(s.st, 1)
                    project_z(i, 1)
                    if group is not None:
                        out_blocks(group, blocks[0:2])
                    if projects:
                        e.wait_ge(s.szr, START + n + 1)
                        project_x(i + 4, 0)
                    if group is not None:
                        out_blocks(group, blocks[2:4])
                    e.wait_ge(s.mt_r, START + 2 * n + 2)
                    e.wait_ge(s.sin, START + n + 1)
                    both_parts(i, 0)
                    if not last:
                        transpose_x(i + 1)
                    if projects:
                        project_x(i + 4, 1)
                    both_parts(i, 1)

                transpose_x(0)
                pair(0, 0)
                pair(1, 1)
                with e.Fori(1, GROUPS - 1) as k:
                    pair(2 * k, 0, group=k - 1)
                    pair(2 * k + 1, 1, group=k - 1)
                pair(PAIRS - 2, 0, group=GROUPS - 2, projects=False)
                pair(PAIRS - 1, 1, group=GROUPS - 2, projects=False, last=True)
                out_blocks(GROUPS - 1, range(NB))
                e.wait_ge(s.ssq, START + 2 * (h * PAIRS + PAIRS))
                for b in range(NB):
                    ins = e.matmul(psy[:, 0, b:b + 1], sumsq[:, b * P:(b + 1) * P], ones[:, 0:1],
                                   start=True, stop=True)
                ins.then_inc(s.ss_mm, 1)
                edge(e, h, 4)
                transpose_norm(1)
                edge(e, h, 5)

                def down(n):
                    for b in range(NB):
                        if b == 0:
                            e.wait_ge(s.hdlo, START + n + 1)
                            e.wait_ge(s.wd_lo, n + 1)
                            e.wait_ge(s.facc, START + NB * n)
                        if b >= 2:
                            e.wait_ge(s.facc, START + NB * n + b - 1)
                        t = slice(b * P, (b + 1) * P)
                        mm3(e, pso[:, b % 2, :], g_hi[:, 0, t], g_lo[:, 0, t], w_hi[:, O, :], w_lo[:, O, :],
                            True, True) \
                            .then_inc(s.fp, 1)

                def up_gate(t):
                    n = h * FT + t
                    e.wait_ge(s.wg_lo, n + 1)
                    e.wait_ge(s.gh, START + n)
                    project(psx[:, 0, :], Z, 0, None)
                    project(psx[:, 1, :], Z, 1, s.gp)
                    e.wait_ge(s.wu_lo, n + 1)
                    e.wait_ge(s.hd, START + n)
                    project(pst[:, 0, :], X, 0, None)
                    project(pst[:, 1, :], X, 1, s.up)

                up_gate(0)
                with e.Fori(1, FT) as t:
                    up_gate(t)
                    down(h * FT + t - 1)
                down(h * FT + FT - 1)

        @block.vector
        def _(e):
            start_counters(e, s.mt_r, s.y_read, s.taps, s.xs, s.szr, s.hd, s.sin, s.oacc, s.facc)
            st = Steps(e, s.dve_step)
            flat = lambda t: t[:, :, :].rearrange("p b k -> p (b k)")
            e.memset(ones[:, :], 1.0).then_inc(s.const_ok, 1)
            e.memset(halo[:, :, :], 0.0)
            e.memset(carry[:, :, :], 0.0)
            e.wait_ge(s.const_in, 16 * 12)
            e.wait_ge(s.mod_c, 3)
            e.scalar_tensor_tensor(out=c_silu[:, :], in0=c_tanh[:, :], scalar=1.0, in1=c_half[:, :],
                                   op0=ALU.add, op1=ALU.mult).then_inc(s.mod_s, 1)
            e.wait_ge(s.mod_s, 1)
            for k in range(KT):
                ins = e.tensor_copy(xdt[:, k, :], c_silu[:, k:k + 1].broadcast_to([P, P]))
            ins.then_inc(s.mod_sb, 1)
            e.tensor_scalar(flat(conv_w), flat(conv_w), 0.5, None, ALU.mult)
            e.tensor_scalar(conv_b[:, :], conv_b[:, :], 0.5, None, ALU.mult)
            e.tensor_scalar(ffn_gs[:, :], ffn_gs[:, :], 0.5, None, ALU.mult)
            e.wait_ge(s.wdt_hi, 1)
            e.tensor_tensor(wdt_lo[:, :, :], wdt_raw, wdt_hi[:, :, :].bitcast(F32), ALU.subtract) \
                .then_inc(s.wdt_lo, 1)
            e.wait_ge(s.wm_used, 6)
            st.mark(e.tensor_copy(mod_col[:, :, :].rearrange("p m k -> p (m k)"), psy[:, 0, 0:4 * KT]))
            for k, row in enumerate((gate_a, gate_b)):
                st.mark(e.tensor_copy(row[:, :], pso[:, k, :]))
                st.sync()
                st.link(e.tensor_scalar(xs[:, 0:HID], row[:, :], 0.0, 2.0, ALU.is_ge, ALU.mult))
                st.link(e.scalar_tensor_tensor(out=xs[:, 512:512 + HID], in0=row[:, :], scalar=-1.0, in1=row[:, :],
                                               op0=ALU.mult, op1=ALU.max))
                st.link(e.tensor_scalar(xs[:, 512:512 + HID], xs[:, 512:512 + HID], 0.25, None, ALU.max))
                st.link(e.scalar_tensor_tensor(out=row[:, :], in0=xs[:, 0:HID], scalar=-1.0,
                                               in1=xs[:, 512:512 + HID], op0=ALU.add, op1=ALU.mult))
            st.link(e.tensor_tensor(gate_b[:, :], gate_b[:, :], g[:, 0:HID], ALU.mult))
            for m in (1, 3):
                st.link(e.tensor_scalar(mod_col[:, m, :], mod_col[:, m, :], 1.0, None, ALU.add))
            assert st.count == DVE_STEPS["setup"], ("setup", st.count)

            with e.Fori(0, HALVES) as h:
                st.base, st.count = h * DVE_STEPS["half"] + DVE_STEPS["setup"], 0
                done = [0]

                def reciprocal_root(k):
                    e.wait_ge(s.root_r, 3 * h + k + 1)
                    st.link(e.reciprocal(rstd[:, :], root[:, :]))
                    st.link(e.tensor_tensor(root[:, :], rstd[:, :], rstd[:, :], ALU.mult))
                    st.link(e.tensor_tensor(root[:, :], root[:, :], var[:, :], ALU.mult))
                    st.link(e.tensor_scalar(root[:, :], root[:, :], -0.5, 1.5, ALU.mult, ALU.add))
                    st.link(e.tensor_tensor(rstd[:, :], rstd[:, :], root[:, :], ALU.mult))

                def layer_norm(which, k):
                    if which == 0:
                        e.wait_ge(s.x_in, 16 * (h + 1))
                    for b in range(NB):
                        st.mark(e.bn_stats(stat[:, b, :], acc[:, b, :]))
                    wait_alone(e, st.sem, st.base + st.count)
                    for b in range(NB):
                        st.mark(e.bn_aggr(mv[:, b, :], stat[:, b, :]))
                    st.sync()
                    e.tensor_scalar(var[:, :], mv[:, :, 1:2].rearrange("p b a -> p (b a)"), LN_EPS, None, ALU.add) \
                        .then_inc(s.var_r, 1)
                    reciprocal_root(k)
                    for b in range(NB):
                        n = (2 * h + which) * NB + b
                        if b >= 2:
                            e.wait_ge(s.tp, n - 1)
                        e.tensor_scalar(xn[:, b % 2, :], acc[:, b, :], mv[:, b, 0:1], rstd[:, b:b + 1],
                                        ALU.subtract, ALU.mult).then_inc(s.xn, 1)
                        if b >= 1:
                            split_h(which, b - 1)
                    split_h(which, NB - 1)

                def split_h(which, b):
                    u, n = b % 2, (2 * h + which) * NB + b
                    e.wait_ge(s.h32, n + 1)
                    t = slice(b * P, (b + 1) * P)
                    st.link(e.tensor_copy(ht_hi[:, :, t], h32[:, u]))
                    e.tensor_tensor(ht_lo[:, :, t], h32[:, u], ht_hi[:, :, t].bitcast(F32), ALU.subtract) \
                        .then_inc(s.ht, 1)

                edge(e, h, 1)
                layer_norm(0, 0)
                edge(e, h, 2)

                def tap(j, k):
                    m = h * TILES + j
                    if k == 0:
                        e.wait_ge(s.tap0, m + 1)
                    else:
                        e.wait_ge(s.tap_k, 2 * m + k)
                    e.scalar_tensor_tensor(
                        out=conv[:, :], in0=xraw[:, k:k + TH],
                        scalar=conv_w[:, bass.ds(j, 1), k:k + 1].rearrange("p a k -> p (a k)"),
                        in1=conv[:, :], op0=ALU.mult, op1=ALU.add).then_inc(s.tap_k if k < TAPS - 2 else s.taps, 1)

                def silu_x(j, dst):
                    m = h * TILES + j
                    e.wait_ge(s.thc, m + 1)
                    e.scalar_tensor_tensor(out=dst, in0=conv_th[:, :], scalar=1.0, in1=conv[:, :],
                                           op0=ALU.add, op1=ALU.mult).then_inc(s.xs, 1)

                def convolve(j, dst):
                    for k in range(TAPS - 1):
                        tap(j, k)
                    silu_x(j, dst)

                convolve(0, b_t[:, :])
                convolve(1, c_t[:, :])
                convolve(2, xs[:, :])
                e.wait_ge(s.btok_tp, h + 1)
                e.tensor_copy(b_tok[:, :, :], pst_b[:, :, :]).then_inc(s.btok, 1)
                e.wait_ge(s.cb_mm, h + 1)
                e.tensor_tensor(cb[:, :, :], pst_b[:, :, :], tri[:, :].unsqueeze(1).broadcast_to([P, NB, P]),
                                ALU.mult).then_inc(s.cb_ok, 1)
                v, ab, ee, uu, lg = (x_skip[:, 0:512], conv_th[:, 0:512], conv_th[:, 512:1024], z_th[:, 0:512],
                                     z_th[:, 512:1024])
                d, zero = g[:, 0:512], g[:, 512:1024]
                e.wait_ge(s.dt_mm, h + 1)
                st.link(e.tensor_tensor(v.rearrange("p (b k) -> p b k", b=NB),
                                        psy[:, 0, :].rearrange("p (b k) -> p b k", b=NB),
                                        dt_bias[:, :].unsqueeze(1).broadcast_to([P, NB, HEADS]), ALU.add))
                e.scalar_tensor_tensor(out=ab, in0=v, scalar=-1.0, in1=v, op0=ALU.mult, op1=ALU.max) \
                    .then_inc(s.dt_abs, 1)
                e.wait_ge(s.dt_exp, h + 1)
                e.tensor_scalar(uu, ee, 1.0, None, ALU.add).then_inc(s.dt_u, 1)
                e.wait_ge(s.dt_u, h + 1)
                st.link(e.tensor_scalar(d, uu, -1.0, None, ALU.add))
                st.link(e.tensor_scalar(zero, d, 0.0, None, ALU.is_equal))
                st.link(e.tensor_tensor(d, d, zero, ALU.add))
                st.link(e.reciprocal(d, d))
                st.link(e.tensor_tensor(d, d, ee, ALU.mult))
                e.wait_ge(s.dt_ln, h + 1)
                st.link(e.tensor_tensor(d, d, lg, ALU.mult))
                st.link(e.tensor_tensor(zero, zero, ee, ALU.mult))
                st.link(e.tensor_tensor(d, d, zero, ALU.add))
                st.link(e.scalar_tensor_tensor(out=d, in0=v, scalar=0.0, in1=d, op0=ALU.max, op1=ALU.add))
                st.link(e.tensor_scalar(flat(dt), d, 0.0, DT_MAX, ALU.max, ALU.min))
                e.scalar_tensor_tensor(out=dt_end[:, :, :], in0=dt[:, :, :], scalar=-1.0,
                                       in1=exp_a[:, :].unsqueeze(1).broadcast_to([P, NB, HEADS]),
                                       op0=ALU.mult, op1=ALU.mult).then_inc(s.dta, 1)
                e.wait_ge(s.cs_mm, h + 1)
                e.tensor_copy(flat(cs), psy[:, 0, :]).then_inc(s.cs_sb, 1)
                e.wait_ge(s.cs_sb, h + 1)
                st.link(e.tensor_tensor(flat(dt_end), psy[:, 1, :], flat(cs), ALU.subtract))
                e.tensor_scalar(flat(dt_end), flat(dt_end), 0.0, None, ALU.min).then_inc(s.csm, 1)
                e.wait_ge(s.dec, 2 * h + 2)
                e.tensor_tensor(flat(dt_end), flat(dt_end), flat(dt), ALU.mult)
                edge(e, h, 3)

                def accumulate(n, blocks, fresh, src_done, dst, done):
                    for b in blocks:
                        e.wait_ge(src_done, START + NB * n + b + 1)
                        if fresh:
                            ins = e.tensor_copy(dst[:, b, :], pso[:, b % 2, :])
                        else:
                            ins = e.tensor_tensor(dst[:, b, :], pso[:, b % 2, :], dst[:, b, :], ALU.add)
                        ins.then_inc(done, 1)

                def heads(table, i, blocks=NB):
                    return table[:, :, bass.ds(2 * i, 2)].unsqueeze(3).broadcast_to([P, NB, 2, HEAD_P])

                four = "p b (r q) -> p b r q"

                def combine(i, q):
                    n = h * PAIRS + i
                    c = slice(q * 512, q * 512 + 512)
                    if q == 0:
                        e.wait_ge(s.erow_in, 32 * (n + 1))
                    e.wait_ge(s.yp, START + 2 * n + q + 1)
                    if not (isinstance(i, int) and i == 0):
                        e.wait_ge(s.ssq, START + 2 * n - 1 + q)
                    st.link(e.tensor_tensor(g[:, c], psy[:, 1, :], e_row[:, c], ALU.mult))
                    e.tensor_tensor(g[:, c], psy[:, 0, :], g[:, c], ALU.add).then_inc(s.y_read, 1)

                def gate(i, q):
                    n = h * PAIRS + i
                    c = slice(q * 512, q * 512 + 512)
                    e.wait_ge(s.y_skip, START + 2 * n + q + 1)
                    e.tensor_tensor(g[:, c], g[:, c], sz[:, c], ALU.mult).then_inc(s.g_r, 1)

                def decayed_x(i):
                    e.wait_ge(s.xT, h * PAIRS + i + 1)
                    e.tensor_tensor(xd[:, :, :].rearrange(four, r=2), pst_b[:, :, :].rearrange(four, r=2),
                                    heads(dt_end, i), ALU.mult).then_inc(s.xd_r, 1)

                def pair(i, parity, first=False, group=None, fresh=False, convolves=True):
                    n = h * PAIRS + i
                    work = []

                    def take(b):
                        if group is not None:
                            accumulate(h * GROUPS + group, [4 * parity + b], fresh, s.op, acc, s.oacc)

                    def state(b):
                        for r in range(2):
                            hp = slice(r * HEAD_P, (r + 1) * HEAD_P)
                            dst = s_in[:, b + 1, hp] if b < NB - 1 else \
                                carry[:, bass.ds(i, 1), hp].rearrange("p a n -> p (a n)")
                            ins = e.scalar_tensor_tensor(out=dst, in0=s_in[:, b, hp],
                                                         scalar=e_last[:, b, bass.ds(2 * i + r, 1)],
                                                         in1=pst_b[:, b, hp], op0=ALU.mult, op1=ALU.add)
                            if b < NB - 1:
                                st.mark(ins)
                        if b == NB - 1:
                            ins.then_inc(s.sin, 1)
                        return st.base + st.count

                    def decay(r):
                        e.wait_ge(s.ex, 2 * n + r + 1)
                        e.tensor_tensor(mt[:, r, :], cs_row[:, r, :], cb[:, :, :].rearrange("p b t -> p (b t)"),
                                        ALU.mult).then_inc(s.mt_r, 1)

                    def silu_z():
                        e.wait_ge(s.thz, n + 1)
                        e.scalar_tensor_tensor(out=sz[:, :], in0=z_th[:, :], scalar=1.0,
                                               in1=psx[:, :, :].rearrange("p a n -> p (a n)"),
                                               op0=ALU.add, op1=ALU.mult).then_inc(s.szr, 1)

                    e.wait_ge(s.yp, START + 2 * n)
                    e.tensor_tensor(xdt[:, :, :].rearrange(four, r=2), pst_b[:, :, :].rearrange(four, r=2),
                                    heads(dt, i), ALU.mult).then_inc(s.xdt_r, 1)
                    st.mark(e.tensor_copy(s_in[:, 0, :], carry[:, bass.ds(i, 1), :].rearrange("p a n -> p (a n)")))
                    if not first:
                        combine(i - 1, 1)
                        gate(i - 1, 0)
                    if convolves:
                        tap(i + 3, 0)
                    st.sync()
                    e.wait_ge(s.st, n + 1)
                    fill = {
                        0: lambda: None if first else gate(i - 1, 1),
                        1: lambda: tap(i + 3, 1) if convolves else None,
                        2: lambda: decay(0),
                        3: silu_z,
                        4: lambda: take(0),
                        5: lambda: take(1),
                        6: lambda: decay(1),
                    }
                    for b in range(NB):
                        seen = state(b)
                        if b < NB - 1:
                            fill[b]()
                            e.wait_ge(st.sem, seen)
                    if convolves:
                        tap(i + 3, 2)
                    take(2)
                    take(3)
                    if convolves:
                        e.wait_ge(s.x_skip, n + 1)
                        silu_x(i + 3, xs[:, :])
                    combine(i, 0)
                    if convolves:
                        decayed_x(i + 1)

                decayed_x(0)
                pair(0, 0, first=True)
                pair(1, 1)
                pair(2, 0, group=0, fresh=True)
                pair(3, 1, group=0, fresh=True)
                at, base = st.count, st.base
                with e.Fori(2, GROUPS - 1) as k:
                    st.base, st.count = base + (k - 2) * DVE_STEPS["pair"] + at, 0
                    pair(2 * k, 0, group=k - 1)
                    pair(2 * k + 1, 1, group=k - 1)
                    assert st.count == DVE_STEPS["pair"], ("pair", st.count)
                st.base, st.count = base, at + (GROUPS - 3) * DVE_STEPS["pair"]
                pair(PAIRS - 2, 0, group=GROUPS - 2)
                pair(PAIRS - 1, 1, group=GROUPS - 2, convolves=False)
                combine(PAIRS - 1, 1)
                for q in range(2):
                    gate(PAIRS - 1, q)
                accumulate(h * GROUPS + GROUPS - 1, range(NB), False, s.op, acc, s.oacc)
                e.wait_ge(s.ss_mm, h + 1)
                e.tensor_scalar(var[:, :], psy[:, 0, 0:NB], 1.0 / (4 * INTER), RMS_EPS, ALU.mult, ALU.add) \
                    .then_inc(s.var_r, 1)
                edge(e, h, 4)
                reciprocal_root(1)
                st.link(e.tensor_scalar(rstd[:, :], rstd[:, :], 0.5, None, ALU.mult))
                for b in range(NB):
                    st.link(e.scalar_tensor_tensor(out=acc[:, b, :], in0=acc[:, b, :], scalar=rstd[:, b:b + 1],
                                                   in1=gate_a[:, :], op0=ALU.mult, op1=ALU.mult))
                    e.wait_ge(s.xres_in[b % 2], 16 * (h * NB // 2 + b // 2 + 1))
                    e.tensor_tensor(acc[:, b, :], acc[:, b, :], x_skip[:, (b % 2) * HID:(b % 2 + 1) * HID], ALU.add) \
                        .then_inc(s.x2, 1)
                e.wait_ge(s.x2, h * NB + NB)
                layer_norm(1, 2)
                edge(e, h, 5)

                def ffn(t, first, fresh):
                    n = h * FT + t
                    e.wait_ge(s.thg, n + 1)
                    st.link(e.scalar_tensor_tensor(out=conv_th[:, :], in0=conv_th[:, :], scalar=1.0, in1=conv[:, :],
                                                   op0=ALU.add, op1=ALU.mult))
                    e.wait_ge(s.up, START + n + 1)
                    e.wait_ge(s.hdlo, START + n)
                    e.scalar_tensor_tensor(out=g[:, :], in0=pst[:, :, :].rearrange("p a n -> p (a n)"),
                                           scalar=ffn_us[:, bass.ds(t, 1)], in1=conv_th[:, :],
                                           op0=ALU.mult, op1=ALU.mult).then_inc(s.hd, 1)
                    if not first:
                        accumulate(n - 1, range(NB), fresh, s.fp, f_acc, s.facc)

                ffn(0, True, False)
                ffn(1, False, True)
                at, base = st.count, st.base
                with e.Fori(2, FT) as t:
                    st.base, st.count = base + (t - 2) * DVE_STEPS["ffn"] + at, 0
                    ffn(t, False, False)
                    assert st.count == DVE_STEPS["ffn"], ("ffn", st.count)
                st.base, st.count = base, at + (FT - 2) * DVE_STEPS["ffn"]
                n = h * FT + FT - 1
                for b in range(NB):
                    accumulate(n, [b], False, s.fp, f_acc, s.facc)
                    e.wait_ge(s.facc, START + NB * n + b + 1)
                    st.link(e.tensor_tensor(f_acc[:, b, :], f_acc[:, b, :], gate_b[:, :], ALU.mult))
                    e.tensor_tensor(acc[:, b, :], acc[:, b, :], f_acc[:, b, :], ALU.add).then_inc(s.fin, 1)
                assert st.count == DVE_STEPS["half"], ("half", st.count)

        @block.gpsimd
        def _(e):
            start_counters(e, s.wx_lo, s.wz_lo, s.wo_lo, s.ssq, s.hdlo, s.y_skip, s.seg)
            e.memset(ident[:, :], 0.0).then_inc(s.const_ok, 1)
            e.memset(tri[:, :], 1.0).then_inc(s.const_ok, 1)
            e.wait_ge(s.const_ok, 3)
            e.affine_select(out=ident[:, :], in_=ident[:, :], compare_op=ALU.not_equal, fill=1.0, base=0,
                            pattern=[[-1, P]], channel_multiplier=1).then_inc(s.const_ok, 1)
            e.affine_select(out=tri[:, :], in_=tri[:, :], compare_op=ALU.is_ge, fill=0.0, base=0,
                            pattern=[[1, P]], channel_multiplier=-1).then_inc(s.const_ok, 1)
            with e.Fori(0, HALVES) as h:
                edge(e, h, 1)
                edge(e, h, 2)

                def low(k, hi_done, count, done, to=None):
                    to = k if to is None else to
                    e.wait_ge(hi_done, count)
                    e.tensor_tensor(w_lo[:, to, :], w_raw[:, k, :], w_hi[:, to, :].bitcast(F32), ALU.subtract) \
                        .then_inc(done, 1)

                for j in range(4):
                    low(X, s.wx_hi, h * TILES + j + 1, s.wx_lo)
                low(Z, s.wz_hi, h * PAIRS + 1, s.wz_lo)
                e.memset(sumsq[:, :], 0.0)
                edge(e, h, 3)

                def skip(i, q):
                    n = h * PAIRS + i
                    c = slice(q * 512, q * 512 + 512)
                    if q == 0:
                        e.wait_ge(s.x_skip, n + 1)
                    e.wait_ge(s.y_read, START + 2 * n + q + 1)
                    e.tensor_tensor(g[:, c], g[:, c], x_skip[:, c], ALU.add).then_inc(s.y_skip, 1)

                def rest(i, parity, q):
                    n = h * PAIRS + i
                    c = slice(q * 512, q * 512 + 512)
                    e.wait_ge(s.ghi, 2 * n + q + 1)
                    e.tensor_tensor(g_lo[:, parity, c], g[:, c], g_hi[:, parity, c].bitcast(F32), ALU.subtract) \
                        .then_inc(s.glo, 1)

                def add_squares(i, q):
                    n = h * PAIRS + i
                    c = slice(q * 512, q * 512 + 512)
                    e.wait_ge(s.sqr, 2 * n + q + 1)
                    e.tensor_tensor(sumsq[:, c], sumsq[:, c], g[:, c], ALU.add).then_inc(s.ssq, 1)

                def blocks(row):
                    return row.rearrange("p (b t) -> p b t", b=NB)

                def cs_s(i, r):
                    return cs[:, :, bass.ds(2 * i + r, 1)].broadcast_to([P, NB, P])

                def exponents(i):
                    n = h * PAIRS + i
                    for r in range(2):
                        e.wait_ge(s.csrow_in[r], 16 * (n + 1))
                        e.tensor_tensor(blocks(cs_row[:, r, :]), blocks(cs_row[:, r, :]), cs_s(i, r),
                                        ALU.subtract).then_inc(s.seg, 1)

                def pair(i, parity, first=False, convolves=True, projects=True):
                    n = h * PAIRS + i
                    if projects:
                        low(X, s.wx_hi, h * TILES + i + 5, s.wx_lo)
                    if not first:
                        if parity == 0:
                            low(O, s.wo_hi, n, s.wo_lo, O + 1)
                        skip(i - 1, 1)
                        rest(i - 1, 1 - parity, 0)
                        if parity == 0:
                            rest(i - 1, 1, 1)
                        add_squares(i - 1, 0)
                        if parity == 0:
                            add_squares(i - 1, 1)
                    if convolves:
                        low(Z, s.wz_hi, n + 2, s.wz_lo)
                    if parity == 1:
                        rest(i - 1, 0, 1)
                        add_squares(i - 1, 1)
                    if convolves:
                        exponents(i + 1)
                    if parity == 1:
                        low(O, s.wo_hi, n, s.wo_lo, O)
                    skip(i, 0)

                exponents(0)
                pair(0, 0, first=True)
                pair(1, 1)
                with e.Fori(1, GROUPS - 1) as k:
                    pair(2 * k, 0)
                    pair(2 * k + 1, 1)
                pair(PAIRS - 2, 0, projects=False)
                pair(PAIRS - 1, 1, convolves=False, projects=False)
                skip(PAIRS - 1, 1)
                for q in range(2):
                    rest(PAIRS - 1, 1, q)
                low(O, s.wo_hi, h * PAIRS + PAIRS, s.wo_lo, O + 1)
                for q in range(2):
                    add_squares(PAIRS - 1, q)
                edge(e, h, 4)
                edge(e, h, 5)
                with e.Fori(0, FT) as t:
                    n = h * FT + t
                    low(Z, s.wg_hi, n + 1, s.wg_lo)
                    low(X, s.wu_hi, n + 1, s.wu_lo)
                    low(O, s.wd_hi, n + 1, s.wd_lo)
                    e.wait_ge(s.hdhi, n + 1)
                    e.tensor_tensor(g_lo[:, 0, :], g[:, :], g_hi[:, 0, :].bitcast(F32), ALU.subtract) \
                        .then_inc(s.hdlo, 1)


def tiles(w, n):
    return np.ascontiguousarray(w.reshape(KT, P, n, P).transpose(2, 1, 0, 3).reshape(n, P, KT * P))


def kernel(**inputs):
    import concourse.bacc as bacc
    from concourse.bass_utils import run_bass_kernel_spmd

    v = {k: np.asarray(x) for k, x in inputs.items()}
    w_in = v["L0_attn_W_in"]
    conv_dim = INTER + 2 * STATE
    w_z, w_xbc, w_dt = w_in[:, :INTER], w_in[:, INTER:INTER + conv_dim], w_in[:, INTER + conv_dim:]

    def bc_first(t):
        return np.concatenate([t[..., INTER:], t[..., :INTER]], axis=-1)

    def col(t, n):
        return np.ascontiguousarray(t.reshape(n, P).T)

    arrays = {
        "x": v["L0_attn_hidden_states"].reshape(TOKENS, HID),
        "wx": tiles(bc_first(w_xbc), TILES),
        "wz": tiles(w_z, PAIRS),
        "wdt": w_dt.reshape(KT, P, HEADS).transpose(1, 0, 2),
        "wo": v["L0_attn_W_out"].reshape(PAIRS, P, HID),
        "conv_w": bc_first(v["L0_attn_conv_w"]).reshape(TAPS, TILES, P).transpose(2, 1, 0),
        "conv_b": col(bc_first(v["L0_attn_conv_b"]), TILES),
        "dt_bias": v["L0_attn_dt_bias"], "a_log": v["L0_attn_A_log"],
        "d": v["L0_attn_D"].reshape(PAIRS, 2).T,
        "norm_w": col(v["L0_attn_norm_weight"], PAIRS),
        "wg": tiles(v["L0_ffn_gate_w"].T, FT), "wu": tiles(v["L0_ffn_up_w"].T, FT),
        "wd": v["L0_ffn_down_w"].T.reshape(FT, P, HID),
        "gate_s": col(v["L0_ffn_gate_s"], FT), "up_s": col(v["L0_ffn_up_s"], FT),
        "down_s": v["L0_ffn_down_s"],
        "c": col(v["L0_c"], KT), "wmod": v["L0_wmod"],
    }
    arrays = {f"in_{k}": np.ascontiguousarray(t) for k, t in arrays.items()}
    nc = bacc.Bacc("TRN2", target_bir_lowering=False, num_devices=1)
    aps = {k[3:]: nc.dram_tensor(k, t.shape, mybir.dt.from_np(t.dtype), kind="ExternalInput").ap()
           for k, t in arrays.items()}
    out = nc.dram_tensor("out", (TOKENS, HID), F32, kind="ExternalOutput").ap()
    build(nc, aps, out)
    r = run_bass_kernel_spmd(nc, [arrays], core_ids=[0])
    return np.asarray(r.results[0]["out"]).reshape(1, TOKENS, HID)
```

```python
from contextlib import ExitStack

import numpy as np

import concourse.bass as bass
from concourse import mybir

F32 = mybir.dt.float32
F32R = mybir.dt.float32r
ALU = mybir.AluOpType
ACT = mybir.ActivationFunctionType

P = 128
TOKENS, HID = 2048, 512
HEADS, HEAD_P, STATE = 64, 64, 128
INTER = HEADS * HEAD_P
KT = HID // P
HALVES = 2
TH = TOKENS // HALVES
NB = TH // P
BANKS = TH // 512
PAIRS = INTER // P
GROUPS = PAIRS // 2
TILES = PAIRS + 2
TAPS = 4
FFN = 1408
FT = FFN // P
LN_EPS = RMS_EPS = 1e-5
DT_MAX = 100.0
EDGES = 2
ENGINES = 5
START = 5

DVE_STEPS = dict(setup=35, half=620, pair=34, ffn=1)


class Steps:

    def __init__(self, engine, sem):
        self.engine, self.sem, self.base, self.count = engine, sem, 0, 0

    def mark(self, ins):
        ins.then_inc(self.sem, 1)
        self.count += 1

    def sync(self):
        self.engine.wait_ge(self.sem, self.base + self.count)

    def link(self, ins):
        self.mark(ins)
        self.sync()


class Semaphores:

    def __init__(self, sem):
        self.edge = sem("edge")
        self.passed = sem("passed")
        self.c_in = sem("c_in")
        self.const_in = sem("const_in")
        self.const_ok = sem("const_ok")
        self.dve_step = sem("dve_step")
        self.wm_used = sem("wm_used")
        self.mod_c = sem("mod_c")
        self.mod_s = sem("mod_s")
        self.mod_sb = sem("mod_sb")
        self.mod_row = sem("mod_row")
        self.mod_cols = sem("mod_cols")
        self.xn = sem("xn")
        self.tp = sem("tp")
        self.h32 = sem("h32")
        self.ht_up = sem("ht_up")
        self.ht = sem("ht")
        self.wdt_hi = sem("wdt_hi")
        self.wdt_lo = sem("wdt_lo")
        self.dt_mm = sem("dt_mm")
        self.dt_heads = sem("dt_heads")
        self.dt_tp = sem("dt_tp")
        self.dt_abs = sem("dt_abs")
        self.dt_exp = sem("dt_exp")
        self.dt_u = sem("dt_u")
        self.dt_ln = sem("dt_ln")
        self.dta = sem("dta")
        self.cs_mm = sem("cs_mm")
        self.cs_sb = sem("cs_sb")
        self.csm = sem("csm")
        self.dec = sem("dec")
        self.cs_tp = sem("cs_tp")
        self.cs_row_ok = sem("cs_row_ok")
        self.scratch = sem("scratch")
        self.cb_mm = sem("cb_mm")
        self.btok_tp = sem("btok_tp")
        self.btok = sem("btok")
        self.wx_in = sem("wx_in")
        self.wx_hi = sem("wx_hi")
        self.wx_lo = sem("wx_lo")
        self.wz_in = sem("wz_in")
        self.wz_hi = sem("wz_hi")
        self.wz_lo = sem("wz_lo")
        self.wo_wn = sem("wo_wn")
        self.wo_hi = sem("wo_hi")
        self.wo_lo = sem("wo_lo")
        self.xp = sem("xp")
        self.halo_in = sem("halo_in")
        self.halo_out = sem("halo_out")
        self.xev = sem("xev")
        self.tap0 = sem("tap0")
        self.tap_k = sem("tap_k")
        self.taps = sem("taps")
        self.thc = sem("thc")
        self.xs = sem("xs")
        self.zp = sem("zp")
        self.thz = sem("thz")
        self.szr = sem("szr")
        self.xT = sem("xT")
        self.xdt_r = sem("xdt_r")
        self.xd_r = sem("xd_r")
        self.st = sem("st")
        self.sin = sem("sin")
        self.erow_in = sem("erow_in")
        self.seg = sem("seg")
        self.relu = sem("relu")
        self.ex = sem("ex")
        self.mt_r = sem("mt_r")
        self.yp = sem("yp")
        self.y_read = sem("y_read")
        self.x_skip = sem("x_skip")
        self.y_skip = sem("y_skip")
        self.g_r = sem("g_r")
        self.ghi = sem("ghi")
        self.glo = sem("glo")
        self.sqr = sem("sqr")
        self.ssq = sem("ssq")
        self.op = sem("op")
        self.oacc = sem("oacc")
        self.ss_mm = sem("ss_mm")
        self.res = sem("res")
        self.x2 = sem("x2")
        self.var_r = sem("var_r")
        self.root_r = sem("root_r")
        self.wg_in = sem("wg_in")
        self.wg_hi = sem("wg_hi")
        self.wg_lo = sem("wg_lo")
        self.wu_in = sem("wu_in")
        self.wu_hi = sem("wu_hi")
        self.wu_lo = sem("wu_lo")
        self.wd_in = sem("wd_in")
        self.wd_sc = sem("wd_sc")
        self.wd_hi = sem("wd_hi")
        self.wd_lo = sem("wd_lo")
        self.gp = sem("gp")
        self.up = sem("up")
        self.gh = sem("gh")
        self.thg = sem("thg")
        self.hd = sem("hd")
        self.hdhi = sem("hdhi")
        self.hdlo = sem("hdlo")
        self.fp = sem("fp")
        self.facc = sem("facc")
        self.out_ok = sem("out_ok")
        self.wm_in = [sem(f"wm_in{k}") for k in range(4)]
        self.x_in = [sem(f"x_in{k}") for k in range(2)]
        self.wo_in = [sem(f"wo_in{k}") for k in range(2)]
        self.xres_in = [sem(f"xres_in{k}") for k in range(2)]
        self.csrow_in = [sem(f"csrow_in{k}") for k in range(2)]


def build(nc, a, out):
    ctx = ExitStack()
    with ctx:
        def sb(name, shape, dt=F32):
            return ctx.enter_context(nc.sbuf_tensor(name, shape, dt))

        def ps(name, shape):
            return ctx.enter_context(nc.psum_tensor(name, shape, F32))

        def sem(name):
            return ctx.enter_context(nc.semaphore(name))

        ident = sb("ident", [P, P])
        tri = sb("tri", [P, P])
        ones = sb("ones", [P, P])
        c_col = sb("c_col", [P, KT])
        c_half = sb("c_half", [P, KT])
        c_tanh = sb("c_tanh", [P, KT])
        c_silu = sb("c_silu", [P, KT])
        mod_col = sb("mod_col", [P, 4, KT])
        gate_a = sb("gate_a", [P, HID])
        gate_b = sb("gate_b", [P, HID])
        conv_w = sb("conv_w", [P, TILES, TAPS])
        conv_b = sb("conv_b", [P, TILES])
        d_col = sb("d_col", [P, PAIRS])
        norm_col = sb("norm_col", [P, PAIRS])
        ffn_gs = sb("ffn_gs", [P, FT])
        ffn_us = sb("ffn_us", [P, FT])
        dt_bias = sb("dt_bias", [P, HEADS])
        exp_a = sb("exp_a", [P, HEADS])
        ht_hi = sb("ht_hi", [P, KT, TH], F32R)
        ht_lo = sb("ht_lo", [P, KT, TH], F32R)
        acc = sb("acc", [P, NB, HID])
        c_t = sb("c_t", [P, TH])
        b_tok = sb("b_tok", [P, NB, STATE])
        cb = sb("cb", [P, NB, P])
        dt = sb("dt", [P, NB, HEADS])
        cs = sb("cs", [P, NB, HEADS])
        dt_end = sb("dt_end", [P, NB, HEADS])
        e_last = sb("e_last", [P, NB, HEADS])
        halo = sb("halo", [P, TILES, TAPS - 1])
        carry = sb("carry", [P, PAIRS, P])
        sumsq = sb("sumsq", [P, TH])
        big = sb("big", [P, 4, TH])
        cs_row, mt = big[:, 0:2, :], big[:, 2:4, :]
        e_row = sb("e_row", [P, TH])
        xraw = sb("xraw", [P, TAPS - 1 + TH])
        xraw_c = sb("xraw_c", [P, TAPS - 1 + TH])
        conv = sb("conv", [P, TH])
        conv_th = sb("conv_th", [P, TH])
        xs = sb("xs", [P, TH])
        z_th = sb("z_th", [P, TH])
        quad = sb("quad", [P, 4, TH])
        sz = quad[:, 3, :]
        xdt, xd, s_in = (quad[:, k, :].rearrange("p (b n) -> p b n", b=NB) for k in range(3))
        g = sb("g", [P, TH])
        x_skip = sb("x_skip", [P, TH])
        g_hi = sb("g_hi", [P, 2, TH], F32R)
        g_lo = sb("g_lo", [P, 2, TH], F32R)
        X, Z, O = 0, 1, 2
        w_raw = sb("w_raw", [P, 4, 512])
        w_hi = sb("w_hi", [P, 4, 512], F32R)
        w_lo = sb("w_lo", [P, 4, 512], F32R)
        wdt_raw = g[:, 512:512 + KT * HEADS].rearrange("p (k m) -> p k m", k=KT)
        wdt_hi = sb("wdt_hi", [P, KT, HEADS], F32R)
        wdt_lo = sb("wdt_lo", [P, KT, HEADS], F32R)
        stat = sb("stat", [P, NB, 6])
        mv = sb("mv", [P, NB, 2])
        var = sb("var", [P, NB])
        root = sb("root", [P, NB])
        rms = sb("rms", [P, NB])
        rstd = sb("rstd", [P, NB])
        xn = conv_th[:, :].rearrange("p (u n) -> p u n", u=2)
        h32 = [t[:, u * HID:(u + 1) * HID].rearrange("p (k t) -> p k t", k=KT) for t in (z_th, conv) for u in range(2)]
        b_t = sz
        cs_t, ecs_t = xdt[0:HEADS], xd[0:HEADS]
        x_ln = quad[:, :, :].rearrange("p a (b n) -> p (a b) n", n=HID)
        x_res = big[:, :, :].rearrange("p a (b n) -> p (a b) n", n=HID)
        wmod_sb = [x_res[:, 0:4], x_res[:, 4:8], acc[:, 0:4, :], acc[:, 4:8, :]]
        dt_v, dt_ab, dt_ee, dt_uu, dt_lg, dt_d, dt_zero = (x_res[:, k, :] for k in range(7))
        dt_t = g[0:HEADS, :]
        c_rows = e_row[:, 0:KT * P].rearrange("p (k n) -> p k n", k=KT)
        mod_row = [conv[:, 0:512], conv[:, 512:1024], conv_th[:, 0:512], conv_th[:, 512:1024]]

        psx = ps("psx", [P, BANKS, 512])
        pst = ps("pst", [P, BANKS, 512])
        psy = ps("psy", [P, 2, 512])
        pso = ps("pso", [P, 2, 512])
        pst_b = pst[:, :, :].rearrange("p a (b n) -> p (a b) n", n=P)
        conv_c = z_th
        x_banks = [psx, pst, pso, psx]
        x_slots = [3, 1, 2, 0]
        down_banks = [pso[:, 0, :], pso[:, 1, :], psy[:, 0, :], psy[:, 1, :]]
        MOD = (2, 5, 0, 1, 3, 4)

        s = Semaphores(sem)

        scr_cs = nc.dram_tensor("scr_cs", (HALVES, HEADS, TH), F32).ap()
        scr_ecs = nc.dram_tensor("scr_ecs", (HALVES, HEADS, TH), F32).ap()
        x_v = a["x"].rearrange("(h b p) n -> h b p n", h=HALVES, p=P)
        out_v = out.rearrange("(h b p) n -> h b p n", h=HALVES, p=P)
        wmod_v = a["wmod"].rearrange("(k p) (m n) -> m p k n", p=P, n=HID)

        def raw_of(j):
            return xraw_c if isinstance(j, int) and j in (1, 3) else xraw

        def conv_of(j):
            return conv_c if isinstance(j, int) and j == 1 else conv

        def wait_alone(e, which, value):
            e.wait_ge(which, value)
            e.sem_inc(s.passed, 1)

        def start_counters(e, *counters):
            for counter in counters:
                e.sem_inc(counter, START)

        def edge(e, h, k):
            e.drain().then_inc(s.edge, 1)
            wait_alone(e, s.edge, (h * EDGES + k) * ENGINES)

        def mm3(e, dst, w_h, w_l, m_h, m_l, start, stop):
            e.matmul(dst, w_h, m_h, start=start, stop=False)
            e.matmul(dst, w_h, m_l, start=False, stop=False)
            return e.matmul(dst, w_l, m_h, start=False, stop=stop)

        block = ctx.enter_context(nc.Block())

        @block.sync
        def _(e):
            e.dma_start(c_col[:, :], a["c"]).then_inc(s.c_in, 16)
            for c in range(4):
                e.dma_start(wmod_sb[c], wmod_v[MOD[c]]).then_inc(s.wm_in[c], 16)
            consts = [
                (conv_w[:, :, :], a["conv_w"]), (conv_b[:, :], a["conv_b"]),
                (norm_col[:, :], a["norm_w"]), (ffn_gs[:, :], a["gate_s"]), (ffn_us[:, :], a["up_s"]),
                (wdt_raw, a["wdt"]),
                (dt_bias[:, :], a["dt_bias"].partition_broadcast(P)),
                (exp_a[:, :], a["a_log"].partition_broadcast(P)),
                (d_col[0:HEAD_P, :], a["d"][0].partition_broadcast(HEAD_P)),
                (d_col[HEAD_P:P, :], a["d"][1].partition_broadcast(HEAD_P)),
                (g[:, 0:HID], a["down_s"].partition_broadcast(P)),
            ]
            for dst, src in consts:
                e.dma_start(dst, src).then_inc(s.const_in, 16)
            for c in range(4, 6):
                e.wait_ge(s.wm_used, c - 3)
                e.dma_start(wmod_sb[c % 4], wmod_v[MOD[c]]).then_inc(s.wm_in[c % 4], 16)
            with e.Fori(0, HALVES) as h:
                for k in range(2):
                    e.dma_start(x_ln[:, 4 * k:4 * k + 4, :], x_v[h, 4 * k:4 * k + 4].rearrange("b p n -> p b n")) \
                        .then_inc(s.x_in[k], 16)
                for j, used in enumerate((s.wu_lo, s.wg_lo, s.wd_lo)):
                    e.wait_ge(used, START + h * FT)
                    e.dma_start(w_raw[:, j, :], a["wx"][j]).then_inc(s.wx_in, 16)
                edge(e, h, 1)

                def load_x(j, split=None):
                    e.wait_ge(s.wx_lo, START + h * TILES + (j if split is None else split))
                    e.dma_start(w_raw[:, X, :], a["wx"][j]).then_inc(s.wx_in, 16)

                def load_z(i):
                    e.wait_ge(s.wz_lo, START + h * PAIRS + i)
                    e.dma_start(w_raw[:, Z, :], a["wz"][i]).then_inc(s.wz_in, 16)

                def load_o(i, parity):
                    e.wait_ge(s.wo_lo, START + h * PAIRS + i - 1)
                    e.dma_start(w_raw[:, O + parity, :], a["wo"][i]).then_inc(s.wo_in[parity], 16)

                def load_cs(i):
                    e.wait_ge(s.mt_r, START + 2 * (h * PAIRS + i))
                    for r in range(2):
                        e.dma_start(cs_row[:, r, :], scr_cs[h, 2 * i + r].partition_broadcast(P)) \
                            .then_inc(s.csrow_in[r], 16)

                def load_e(i):
                    e.wait_ge(s.y_read, START + 2 * (h * PAIRS + i))
                    for r in range(2):
                        e.dma_start(e_row[r * HEAD_P:(r + 1) * HEAD_P, :],
                                    scr_ecs[h, 2 * i + r].partition_broadcast(HEAD_P)) \
                            .then_inc(s.erow_in, 16)

                load_x(3, 1)
                e.wait_ge(s.wx_lo, START + h * TILES + 2)
                e.dma_start(w_raw[:, Z, :], a["wz"][0]).then_inc(s.wz_in, 16)
                e.wait_ge(s.cs_row_ok, 2 * (h + 1))
                e.dma_start(scr_cs[h], cs_t.rearrange("p b t -> p (b t)")).then_inc(s.scratch, 16)
                e.dma_start(scr_ecs[h], ecs_t.rearrange("p b t -> p (b t)")).then_inc(s.scratch, 16)
                e.wait_ge(s.scratch, 32 * (h + 1))
                load_cs(0)
                load_x(4)
                load_z(1)
                edge(e, h, 2)

                def loads(i, parity, projects=True, convolves=True):
                    load_e(i)
                    if projects and not (isinstance(i, int) and i + 5 >= TILES):
                        load_x(i + 5)
                    load_o(i, parity)
                    if projects:
                        load_z(i + 2)
                    if convolves:
                        load_cs(i + 1)

                with e.Fori(0, GROUPS - 2) as k:
                    loads(2 * k, 0)
                    loads(2 * k + 1, 1)
                loads(PAIRS - 4, 0)
                loads(PAIRS - 3, 1)
                loads(PAIRS - 2, 0, projects=False)
                loads(PAIRS - 1, 1, projects=False, convolves=False)
                e.wait_ge(s.wz_lo, START + (h + 1) * PAIRS)
                e.dma_start(w_raw[:, Z, :], a["wg"][0]).then_inc(s.wg_in, 16)
                e.wait_ge(s.wx_lo, START + (h + 1) * TILES)
                e.dma_start(w_raw[:, X, :], a["wu"][0]).then_inc(s.wu_in, 16)
                e.wait_ge(s.yp, START + 2 * (h + 1) * PAIRS)
                for k in range(2):
                    e.dma_start(x_res[:, 4 * k:4 * k + 4, :], x_v[h, 4 * k:4 * k + 4].rearrange("b p n -> p b n")) \
                        .then_inc(s.xres_in[k], 16)
                e.wait_ge(s.wo_lo, START + (h + 1) * PAIRS)
                e.dma_start(w_raw[:, O, :], a["wd"][0]).then_inc(s.wd_in, 16)
                with e.Fori(0, FT - 1) as t:
                    for k, src, used, done in ((Z, a["wg"], s.wg_lo, s.wg_in), (X, a["wu"], s.wu_lo, s.wu_in),
                                               (O, a["wd"], s.wd_lo, s.wd_in)):
                        e.wait_ge(used, START + h * FT + t + 1)
                        e.dma_start(w_raw[:, k, :], src[t + 1]).then_inc(done, 16)

        @block.scalar
        def _(e):
            start_counters(e, s.gh, s.out_ok, s.halo_out)
            def copy(o, i, **kw):
                return e.activation(o, i, ACT.Copy, **kw)

            e.wait_ge(s.c_in, 16)
            e.activation(c_half[:, :], c_col[:, :], ACT.Copy, scale=0.5).then_inc(s.mod_c, 1)
            e.activation(c_tanh[:, :], c_col[:, :], ACT.Tanh, scale=0.5).then_inc(s.mod_c, 1)
            e.wait_ge(s.const_in, 16 * 11)
            e.activation(exp_a[:, :], exp_a[:, :], ACT.Exp).then_inc(s.mod_c, 1)
            copy(wdt_hi[:, :, :], wdt_raw).then_inc(s.wdt_hi, 1)
            h = 0

            def square_root(k, cols):
                e.wait_ge(s.var_r, 4 * h + k + 1)
                e.activation(root[:, cols], var[:, cols], ACT.Sqrt).then_inc(s.root_r, 1)

            square_root(0, slice(0, NB))
            with e.Fori(0, HALVES) as h:
                edge(e, h, 1)

                def transposed_norm(which, blocks):
                    for b in blocks:
                        n = (2 * h + which) * NB + b
                        e.wait_ge(s.tp, n + 1)
                        if b >= 4:
                            e.wait_ge(s.ht, n - 3)
                        for k in range(KT):
                            ins = e.activation(h32[b % 4][:, k, :], pst[:, b % 2, k * P:(k + 1) * P], ACT.Identity,
                                               scale=mod_col[:, 2 * which + 1, k:k + 1],
                                               bias=mod_col[:, 2 * which, k:k + 1])
                        ins.then_inc(s.h32, 1)

                e.wait_ge(s.wx_in, 16 * (h * TILES + 3))
                for j in range(3):
                    copy(w_hi[:, x_slots[j], :], w_raw[:, j, :]).then_inc(s.wx_hi, 1)
                transposed_norm(0, range(NB))

                def split_x(j):
                    m = h * TILES + j
                    e.wait_ge(s.wx_in, 16 * (m + 1))
                    e.wait_ge(s.xp, START + 2 * m)
                    copy(w_hi[:, X, :], w_raw[:, X, :]).then_inc(s.wx_hi, 1)

                def split_z(i):
                    n = h * PAIRS + i
                    e.wait_ge(s.wz_in, 16 * (n + 1))
                    e.wait_ge(s.zp, START + 2 * n)
                    copy(w_hi[:, Z, :], w_raw[:, Z, :]).then_inc(s.wz_hi, 1)

                def split_o(i, parity):
                    n = h * PAIRS + i
                    e.wait_ge(s.wo_in[parity], 8 * (n - parity) + 16)
                    e.activation(w_raw[:, O + parity, :], w_raw[:, O + parity, :], ACT.Copy,
                                 scale=norm_col[:, bass.ds(i, 1)]).then_inc(s.wo_wn, 1)
                    e.wait_ge(s.wo_wn, n + 1)
                    e.wait_ge(s.op, START + NB // 2 * (n - parity))
                    copy(w_hi[:, O + parity, :], w_raw[:, O + parity, :]).then_inc(s.wo_hi, 1)

                def evacuate_x(j, q):
                    m = h * TILES + j
                    raw = raw_of(j)
                    e.wait_ge(s.xp, START + 2 * m + q + 1)
                    if q == 0:
                        e.wait_ge(s.taps, START + m - (1 if isinstance(j, int) and 1 <= j <= 3 else 0))
                        copy(raw[:, 0:TAPS - 1], halo[:, bass.ds(j, 1), :].rearrange("p a k -> p (a k)")) \
                            .then_inc(s.halo_in, 1)
                    else:
                        e.wait_ge(s.halo_out, START + m)
                    c0 = TAPS - 1 + q * 512
                    bank = x_banks[j] if isinstance(j, int) and j < 4 else psx
                    copy(raw[:, c0:c0 + 512], bank[:, q, :]).then_inc(s.xev, 1)

                def tap_last(j):
                    m = h * TILES + j
                    e.wait_ge(s.xev, 2 * (m + 1))
                    e.wait_ge(s.halo_in, m + 1)
                    raw, dst = raw_of(j), conv_of(j)
                    e.wait_ge(s.xs, START + m - (1 if isinstance(j, int) and 1 <= j <= 2 else 0))
                    e.activation(dst[:, :], raw[:, TAPS - 1:TAPS - 1 + TH], ACT.Identity,
                                 scale=conv_w[:, bass.ds(j, 1), TAPS - 1:TAPS].rearrange("p a k -> p (a k)"),
                                 bias=conv_b[:, bass.ds(j, 1)]).then_inc(s.tap0, 1)
                    copy(halo[:, bass.ds(j, 1), :].rearrange("p a k -> p (a k)"), raw[:, TH:TH + TAPS - 1]) \
                        .then_inc(s.halo_out, 1)

                def silu_tanh(j):
                    m = h * TILES + j
                    src = conv_of(j)
                    e.wait_ge(s.xs, START + m)
                    e.wait_ge(s.taps, START + m + 1)
                    e.activation(conv_th[:, :], src[:, :], ACT.Tanh).then_inc(s.thc, 1)

                e.wait_ge(s.wx_in, 16 * (h * TILES + 4))
                copy(w_hi[:, X, :], w_raw[:, X, :]).then_inc(s.wx_hi, 1)
                e.activation(c_tanh[:, :], ones[:, 0:KT], ACT.Exp)
                e.wait_ge(s.dt_mm, 2 * h + 2)
                copy(dt_t, psy[0:HEADS, :, :].rearrange("p a n -> p (a n)")).then_inc(s.dt_heads, 1)
                evacuate_x(0, 0)
                e.wait_ge(s.dt_abs, h + 1)
                e.activation(dt_ee, dt_ab, ACT.Exp, scale=-1.0).then_inc(s.dt_exp, 1)
                evacuate_x(0, 1)
                tap_last(0)
                e.wait_ge(s.dt_u, h + 1)
                e.activation(dt_lg, dt_uu, ACT.Ln).then_inc(s.dt_ln, 1)
                for q in range(2):
                    evacuate_x(1, q)
                tap_last(1)
                e.wait_ge(s.xp, START + 2 * (h * TILES + 2))
                split_z(0)
                silu_tanh(0)
                for q in range(2):
                    evacuate_x(2, q)
                e.wait_ge(s.csm, h + 1)
                flat = lambda t: t[:, :, :].rearrange("p b k -> p (b k)")
                e.activation(flat(dt_end), flat(dt_end), ACT.Exp).then_inc(s.dec, 1)
                e.activation(flat(e_last), psy[:, 1, :], ACT.Exp).then_inc(s.dec, 1)
                e.wait_ge(s.cs_tp, h + 1)
                copy(cs_t.rearrange("p b t -> p (b t)"), pst[0:HEADS, :, :].rearrange("p a n -> p (a n)")) \
                    .then_inc(s.cs_row_ok, 1)
                e.activation(ecs_t.rearrange("p b t -> p (b t)"), pst[0:HEADS, :, :].rearrange("p a n -> p (a n)"),
                             ACT.Exp).then_inc(s.cs_row_ok, 1)
                tap_last(2)
                e.wait_ge(s.btok_tp, h + 1)
                copy(b_tok[:, :, :], pst_b[:, :, :]).then_inc(s.btok, 1)
                silu_tanh(1)
                for q in range(2):
                    evacuate_x(3, q)
                silu_tanh(2)
                wait_alone(e, s.out_ok, START + 16 * NB * h)
                edge(e, h, 2)

                def round_g(i, parity, q):
                    n = h * PAIRS + i
                    c = slice(q * 512, q * 512 + 512)
                    e.wait_ge(s.g_r, 2 * n + q + 1)
                    e.wait_ge(s.op, START + NB // 2 * (n - parity - 2 * (1 - q)) + 4 * (1 - q)
                              if not isinstance(i, int) or i >= 2 else START + NB // 2 * h * PAIRS)
                    copy(g_hi[:, parity, c], g[:, c]).then_inc(s.ghi, 1)

                def square_g(i, q):
                    n = h * PAIRS + i
                    c = slice(q * 512, q * 512 + 512)
                    e.wait_ge(s.glo, 2 * n + q + 1)
                    e.activation(g[:, c], g[:, c], ACT.Square).then_inc(s.sqr, 1)

                def clip_exponents(n, r):
                    e.wait_ge(s.seg, START + 2 * n + r + 1)
                    e.activation(cs_row[:, r, :], cs_row[:, r, :], ACT.Relu, scale=-1.0).then_inc(s.relu, 1)

                def tanh_z(n, q):
                    c = slice(q * 512, q * 512 + 512)
                    e.wait_ge(s.zp, START + 2 * n + q + 1)
                    e.wait_ge(s.szr, START + 2 * n)
                    e.activation(z_th[:, c], psx[:, q, :], ACT.Tanh, scale=0.5).then_inc(s.thz, 1)

                def exponential(n, r):
                    e.wait_ge(s.relu, 2 * n + r + 1)
                    e.activation(cs_row[:, r, :], cs_row[:, r, :], ACT.Exp, scale=-1.0).then_inc(s.ex, 1)

                def pair(i, parity, first=False, convolves=True, projects=True):
                    n = h * PAIRS + i
                    if convolves:
                        tap_last(i + 3)
                    if projects:
                        split_x(i + 4)
                    tanh_z(n, 0)
                    if not first:
                        round_g(i - 1, 1 - parity, 0)
                    clip_exponents(n, 0)
                    exponential(n, 0)
                    tanh_z(n, 1)
                    e.wait_ge(s.xs, START + h * TILES + i + 3)
                    e.wait_ge(s.y_skip, START + 2 * n)
                    e.activation(x_skip[:, :], xs[:, :], ACT.Copy, scale=d_col[:, bass.ds(i, 1)]) \
                        .then_inc(s.x_skip, 1)
                    clip_exponents(n, 1)
                    exponential(n, 1)
                    if not first:
                        if parity == 0:
                            round_g(i - 1, 1, 1)
                        square_g(i - 1, 0)
                        if parity == 0:
                            square_g(i - 1, 1)
                    if convolves:
                        split_z(i + 1)
                        silu_tanh(i + 3)
                    if projects:
                        evacuate_x(i + 4, 0)
                    if parity == 1:
                        round_g(i - 1, 0, 1)
                        split_o(i - 1, 0)
                        split_o(i, 1)
                        square_g(i - 1, 1)
                    if projects:
                        evacuate_x(i + 4, 1)

                pair(0, 0, first=True)
                pair(1, 1)
                with e.Fori(1, GROUPS - 1) as k:
                    pair(2 * k, 0)
                    pair(2 * k + 1, 1)
                pair(PAIRS - 2, 0, projects=False)
                pair(PAIRS - 1, 1, convolves=False, projects=False)
                for q in range(2):
                    round_g(PAIRS - 1, 1, q)
                for q in range(2):
                    square_g(PAIRS - 1, q)
                n0 = h * FT

                def split_in(t):
                    e.wait_ge(s.wg_in, 16 * (n0 + t + 1))
                    e.wait_ge(s.gp, START + n0 + t)
                    copy(w_hi[:, Z, :], w_raw[:, Z, :]).then_inc(s.wg_hi, 1)
                    e.wait_ge(s.wu_in, 16 * (n0 + t + 1))
                    e.wait_ge(s.up, START + n0 + t)
                    copy(w_hi[:, X, :], w_raw[:, X, :]).then_inc(s.wu_hi, 1)

                e.wait_ge(s.zp, START + 2 * (h + 1) * PAIRS)
                e.wait_ge(s.xp, START + 2 * (h + 1) * TILES)
                split_in(0)
                square_root(1, slice(0, NB))
                square_root(2, slice(0, 4))
                transposed_norm(1, range(2))
                square_root(3, slice(4, 8))
                transposed_norm(1, range(2, NB))
                e.activation(c_tanh[:, :], ones[:, 0:KT], ACT.Tanh)

                def ffn(t, u, last=False):
                    n = n0 + t
                    e.wait_ge(s.gp, START + n + 1)
                    e.wait_ge(s.hd, START + n)
                    e.activation(conv[:, :], psx[:, :, :].rearrange("p a n -> p (a n)"), ACT.Copy,
                                 scale=ffn_gs[:, bass.ds(t, 1)]).then_inc(s.gh, 1)
                    e.wait_ge(s.gh, START + n + 1)
                    e.activation(conv_th[:, :], conv[:, :], ACT.Tanh).then_inc(s.thg, 1)
                    if not last:
                        split_in(t + 1)
                    if isinstance(t, int) and t < 2:
                        e.wait_ge(s.op, START + NB * GROUPS * (h + 1))
                    else:
                        e.wait_ge(s.fp, START + NB * (n - 1))
                    e.wait_ge(s.hd, START + n + 1)
                    copy(g_hi[:, u, :], g[:, :]).then_inc(s.hdhi, 1)
                    e.wait_ge(s.wd_sc, n + 1)
                    copy(w_hi[:, O + u, :], w_raw[:, O, :]).then_inc(s.wd_hi, 1)

                ffn(0, 0)
                with e.Fori(0, (FT - 3) // 2) as k:
                    ffn(2 * k + 1, 1)
                    ffn(2 * k + 2, 0)
                ffn(FT - 2, 1)
                ffn(FT - 1, 0, last=True)
                square_root(4, slice(0, NB))
                for b in range(NB):
                    e.wait_ge(s.facc, START + NB * (n0 + FT - 1) + b + 1)
                    e.dma_start(out_v[h, b], acc[:, b, :]).then_inc(s.out_ok, 16)
            wait_alone(e, s.out_ok, START + 16 * NB * HALVES)

        @block.tensor
        def _(e):
            start_counters(e, s.xp, s.zp, s.op, s.fp, s.yp, s.gp, s.up)
            e.wait_ge(s.const_ok, 5)
            e.wait_ge(s.mod_sb, 1)
            row_banks = [pso[:, 0, :], pso[:, 1, :], psx[:, 0, :], psx[:, 1, :], pst[:, 0, :], pst[:, 1, :]]
            for c in range(7):
                if c < 6:
                    e.wait_ge(s.wm_in[c % 4], 16 * (c // 4 + 1))
                    for k in range(KT):
                        ins = e.matmul(row_banks[c], c_rows[:, k, :], wmod_sb[c % 4][:, k, :],
                                       start=k == 0, stop=k == KT - 1)
                    ins.then_inc(s.wm_used, 1)
                if c >= 3:
                    e.wait_ge(s.mod_row, c - 2)
                    for j in range(KT):
                        col = (c - 3) * KT + j
                        ins = e.matmul(psy[:, 0, col:col + 1], mod_row[c - 3][:, j * P:(j + 1) * P], ident[:, 0:1],
                                       start=True, stop=True)
            ins.then_inc(s.mod_cols, 1)
            with e.Fori(0, HALVES) as h:
                edge(e, h, 1)

                def transpose_norm(which, blocks):
                    for b in blocks:
                        n = (2 * h + which) * NB + b
                        e.wait_ge(s.xn, n + 1)
                        if b >= 2:
                            e.wait_ge(s.h32, n - 1)
                        for k in range(KT):
                            ins = e.transpose(pst[:, b % 2, k * P:(k + 1) * P], xn[:, b % 2, k * P:(k + 1) * P],
                                              ident[:, :])
                        ins.then_inc(s.tp, 1)

                def project(dst, w, q, done):
                    for k in range(KT):
                        c, t = slice(k * P, (k + 1) * P), slice(q * 512, (q + 1) * 512)
                        ins = mm3(e, dst, w_hi[:, w, c], w_lo[:, w, c], ht_hi[:, k, t], ht_lo[:, k, t],
                                  k == 0, k == KT - 1)
                    if done is not None:
                        ins.then_inc(done, 1)
                    return ins

                def project_x(j, q):
                    if q == 0:
                        e.wait_ge(s.wx_lo, START + h * TILES + j + 1)
                    if isinstance(j, int) and j < 4:
                        project(x_banks[j][:, q, :], x_slots[j], q, s.xp)
                    else:
                        project(psx[:, q, :], X, q, s.xp)

                def project_dt(q):
                    e.wait_ge(s.ht, 2 * h * NB + 4 * q + 4)
                    t = slice(q * 512, (q + 1) * 512)
                    for k in range(KT):
                        ins = mm3(e, psy[0:HEADS, q, :], wdt_hi[:, k, :], wdt_lo[:, k, :], ht_hi[:, k, t],
                                  ht_lo[:, k, t], k == 0, k == KT - 1)
                    ins.then_inc(s.dt_mm, 1)

                def project_z(i, q):
                    n = h * PAIRS + i
                    if q == 0:
                        e.wait_ge(s.wz_lo, START + n + 1)
                    if not isinstance(i, int) or i + 3 < TILES:
                        e.wait_ge(s.xev, 2 * (h * TILES + i + 3) + q + 1)
                    project(psx[:, q, :], Z, q, s.zp)

                e.wait_ge(s.wdt_lo, 1)
                transpose_norm(0, range(NB))
                for q in range(2):
                    project_dt(q)
                project_x(0, 0)
                wait_alone(e, s.dt_heads, h + 1)
                for b in range(NB):
                    ins = e.transpose(pso[:, 0, b * HEADS:(b + 1) * HEADS], dt_t[:, b * P:(b + 1) * P],
                                      ident[0:HEADS, 0:HEADS])
                ins.then_inc(s.dt_tp, 1)
                project_x(0, 1)
                for q in range(2):
                    project_x(1, q)
                e.wait_ge(s.dt_abs, h + 1)
                for q in range(2):
                    project_x(2, q)
                e.wait_ge(s.dta, h + 1)
                flat = lambda t: t[:, :, :].rearrange("p b k -> p (b k)")
                e.matmul(psy[:, 0, :], tri[:, :], flat(dt_end), start=True, stop=True)
                e.matmul(psy[:, 1, :], ones[:, :], flat(dt_end), start=True, stop=True).then_inc(s.cs_mm, 1)
                e.wait_ge(s.xev, 2 * (h * TILES + 1))
                project_x(3, 0)
                wait_alone(e, s.xev, 2 * (h * TILES + 2))
                wait_alone(e, s.cs_sb, h + 1)
                for b in range(NB):
                    ins = e.transpose(pst[0:HEADS, b // 4, (b % 4) * P:(b % 4 + 1) * P], cs[:, b, :], ident[:, :])
                ins.then_inc(s.cs_tp, 1)
                project_x(3, 1)
                e.wait_ge(s.xs, START + h * TILES + 1)
                e.wait_ge(s.cs_row_ok, 2 * (h + 1))
                for b in range(NB):
                    ins = e.transpose(pst_b[:, b, :], b_t[:, b * P:(b + 1) * P], ident[:, :])
                ins.then_inc(s.btok_tp, 1)
                project_z(0, 0)
                e.wait_ge(s.xs, START + h * TILES + 2)
                e.wait_ge(s.btok, h + 1)
                for b in range(NB):
                    t = slice(b * P, (b + 1) * P)
                    ins = e.matmul(pst_b[:, b, :], b_t[:, t], c_t[:, t], start=True, stop=True)
                ins.then_inc(s.cb_mm, 1)
                project_z(0, 1)
                edge(e, h, 2)

                def out_blocks(k, blocks):
                    n = h * GROUPS + k
                    for b in blocks:
                        if b % 4 == 0:
                            e.wait_ge(s.glo, 4 * n + 3 + b // 4)
                        if b == 0:
                            e.wait_ge(s.wo_lo, START + 2 * n + 2)
                        e.wait_ge(s.oacc, START + NB * n + b - 1 if b else START + NB * n)
                        t = slice(b * P, (b + 1) * P)
                        for parity in range(2):
                            ins = mm3(e, pso[:, b % 2, :], g_hi[:, parity, t], g_lo[:, parity, t],
                                      w_hi[:, O + parity, :], w_lo[:, O + parity, :], parity == 0, parity == 1)
                        ins.then_inc(s.op, 1)

                def transpose_x(i):
                    n = h * PAIRS + i
                    e.wait_ge(s.xs, START + h * TILES + i + 3)
                    e.wait_ge(s.sin, START + n)
                    for b in range(NB):
                        ins = e.transpose(pst_b[:, b, :], xs[:, b * P:(b + 1) * P], ident[:, :])
                    ins.then_inc(s.xT, 1)

                def both_parts(i, q):
                    n = h * PAIRS + i
                    e.wait_ge(s.y_read, START + 2 * n + q)
                    blocks = range(4 * q, 4 * q + 4)

                    def inside(r):
                        e.wait_ge(s.mt_r, START + 2 * n + r + 1)
                        hp = slice(r * HEAD_P, (r + 1) * HEAD_P)
                        for b in blocks:
                            c = slice((b % 4) * P, (b % 4 + 1) * P)
                            ins = e.matmul(psy[hp, 0, c], xdt[:, b, hp], mt[:, r, b * P:(b + 1) * P],
                                           start=True, stop=True)
                        return ins

                    inside(0)
                    e.wait_ge(s.sin, START + n + 1)
                    for b in blocks:
                        c = slice((b % 4) * P, (b % 4 + 1) * P)
                        e.matmul(psy[:, 1, c], s_in[:, b, :], c_t[:, b * P:(b + 1) * P], start=True, stop=True)
                    ins = inside(1)
                    ins.then_inc(s.yp, 1)

                def pair(i, parity, group=None, projects=True, first=False, last=False):
                    n = h * PAIRS + i
                    blocks = range(4 * parity, 4 * parity + 4)
                    if not first:
                        project_z(i, 0)
                    e.wait_ge(s.xd_r, n + 1)
                    e.wait_ge(s.xdt_r, n + 1)
                    for b in range(NB):
                        ins = e.matmul(pst_b[:, b, :], b_tok[:, b, :], xd[:, b, :], start=True, stop=True)
                    ins.then_inc(s.st, 1)
                    if not first:
                        project_z(i, 1)
                    if group is not None:
                        out_blocks(group, blocks[0:2])
                    if projects:
                        e.wait_ge(s.szr, START + 2 * n + 1)
                        project_x(i + 4, 0)
                    if group is not None:
                        out_blocks(group, blocks[2:4])
                    both_parts(i, 0)
                    if projects:
                        e.wait_ge(s.szr, START + 2 * n + 2)
                        project_x(i + 4, 1)
                    if not last:
                        transpose_x(i + 1)
                    both_parts(i, 1)

                transpose_x(0)
                pair(0, 0, first=True)
                pair(1, 1)
                with e.Fori(1, GROUPS - 1) as k:
                    pair(2 * k, 0, group=k - 1)
                    pair(2 * k + 1, 1, group=k - 1)
                pair(PAIRS - 2, 0, group=GROUPS - 2, projects=False)
                pair(PAIRS - 1, 1, group=GROUPS - 2, projects=False, last=True)
                out_blocks(GROUPS - 1, range(4))
                e.wait_ge(s.ssq, START + 2 * (h * PAIRS + PAIRS))
                for b in range(NB):
                    ins = e.matmul(psy[:, 0, b:b + 1], sumsq[:, b * P:(b + 1) * P], ones[:, 0:1],
                                   start=True, stop=True)
                ins.then_inc(s.ss_mm, 1)
                out_blocks(GROUPS - 1, range(4, NB))

                def down(t, u):
                    n = h * FT + t
                    e.wait_ge(s.hdlo, START + n + 1)
                    e.wait_ge(s.wd_lo, START + n + 1)
                    for b in range(NB):
                        e.wait_ge(s.facc, START + NB * n + b - 3)
                        t = slice(b * P, (b + 1) * P)
                        mm3(e, down_banks[b % 4], g_hi[:, u, t], g_lo[:, u, t], w_hi[:, O + u, :], w_lo[:, O + u, :],
                            True, True) \
                            .then_inc(s.fp, 1)

                def gate_up(t):
                    n = h * FT + t
                    e.wait_ge(s.wg_lo, START + n + 1)
                    e.wait_ge(s.gh, START + n)
                    project(psx[:, 0, :], Z, 0, None)
                    project(psx[:, 1, :], Z, 1, s.gp)
                    up(t)

                def up(t):
                    n = h * FT + t
                    e.wait_ge(s.wu_lo, START + n + 1)
                    e.wait_ge(s.hd, START + n)
                    project(pst[:, 0, :], X, 0, None)
                    project(pst[:, 1, :], X, 1, s.up)

                transpose_norm(1, range(NB))
                e.wait_ge(s.wg_lo, START + h * FT + 1)
                e.wait_ge(s.ht, (2 * h + 1) * NB + 4)
                project(psx[:, 0, :], Z, 0, None)
                e.wait_ge(s.ht, (2 * h + 2) * NB)
                project(psx[:, 1, :], Z, 1, s.gp)
                up(0)
                with e.Fori(0, (FT - 1) // 2) as k:
                    gate_up(2 * k + 1)
                    down(2 * k, 0)
                    gate_up(2 * k + 2)
                    down(2 * k + 1, 1)
                down(FT - 1, 0)

        @block.vector
        def _(e):
            start_counters(e, s.mt_r, s.y_read, s.taps, s.xs, s.szr, s.hd, s.sin, s.oacc, s.facc)
            st = Steps(e, s.dve_step)
            flat = lambda t: t[:, :, :].rearrange("p b k -> p (b k)")
            e.memset(ones[:, :], 1.0).then_inc(s.const_ok, 1)
            e.memset(halo[:, :, :], 0.0)
            e.memset(carry[:, :, :], 0.0)
            e.wait_ge(s.mod_c, 2)
            e.scalar_tensor_tensor(out=c_silu[:, :], in0=c_tanh[:, :], scalar=1.0, in1=c_half[:, :],
                                   op0=ALU.add, op1=ALU.mult).then_inc(s.mod_s, 1)
            e.wait_ge(s.mod_s, 1)
            for k in range(KT):
                ins = e.tensor_copy(c_rows[:, k, :], c_silu[:, k:k + 1].broadcast_to([P, P]))
            ins.then_inc(s.mod_sb, 1)
            e.wait_ge(s.const_in, 16 * 11)
            e.tensor_scalar(flat(conv_w), flat(conv_w), 0.5, None, ALU.mult)
            e.tensor_scalar(conv_b[:, :], conv_b[:, :], 0.5, None, ALU.mult)
            e.tensor_scalar(ffn_gs[:, :], ffn_gs[:, :], 0.5, None, ALU.mult)
            e.wait_ge(s.mod_c, 3)
            e.wait_ge(s.wdt_hi, 1)
            e.tensor_tensor(wdt_lo[:, :, :], wdt_raw, wdt_hi[:, :, :].bitcast(F32), ALU.subtract) \
                .then_inc(s.wdt_lo, 1)
            for k, row in enumerate((gate_a, gate_b)):
                e.wait_ge(s.wm_used, k + 1)
                st.mark(e.tensor_copy(row[:, :], pso[:, k, :]))
                st.sync()
                st.link(e.tensor_scalar(xs[:, 0:HID], row[:, :], 0.0, 2.0, ALU.is_ge, ALU.mult))
                st.link(e.scalar_tensor_tensor(out=xs[:, 512:512 + HID], in0=row[:, :], scalar=-1.0, in1=row[:, :],
                                               op0=ALU.mult, op1=ALU.max))
                st.link(e.tensor_scalar(xs[:, 512:512 + HID], xs[:, 512:512 + HID], 0.25, None, ALU.max))
                st.link(e.scalar_tensor_tensor(out=row[:, :], in0=xs[:, 0:HID], scalar=-1.0,
                                               in1=xs[:, 512:512 + HID], op0=ALU.add, op1=ALU.mult))
            st.link(e.tensor_tensor(gate_b[:, :], gate_b[:, :], g[:, 0:HID], ALU.mult))
            h = 0

            def reciprocal_root(dst, k, cols):
                e.wait_ge(s.root_r, 4 * h + k + 1)
                st.link(e.reciprocal(dst[:, cols], root[:, cols]))
                st.link(e.tensor_tensor(root[:, cols], dst[:, cols], dst[:, cols], ALU.mult))
                st.link(e.tensor_tensor(root[:, cols], root[:, cols], var[:, cols], ALU.mult))
                st.link(e.tensor_scalar(root[:, cols], root[:, cols], -0.5, 1.5, ALU.mult, ALU.add))
                st.link(e.tensor_tensor(dst[:, cols], dst[:, cols], root[:, cols], ALU.mult))

            def statistics(src, blocks):
                for b in blocks:
                    st.mark(e.bn_stats(stat[:, b, :], src[:, b, :]))

            def variances(blocks):
                wait_alone(e, st.sem, st.base + st.count)
                for b in blocks:
                    st.mark(e.bn_aggr(mv[:, b, :], stat[:, b, :]))
                st.sync()
                cols = slice(blocks[0], blocks[-1] + 1)
                e.tensor_scalar(var[:, cols], mv[:, cols, 1:2].rearrange("p b a -> p (b a)"), LN_EPS, None,
                                ALU.add).then_inc(s.var_r, 1)

            for c in range(4):
                e.wait_ge(s.wm_used, c + 3)
                e.tensor_copy(mod_row[c], (psx if c < 2 else pst)[:, c % 2, :]).then_inc(s.mod_row, 1)
                if c >= 2:
                    e.wait_ge(s.x_in[c - 2], 16)
                    statistics(x_ln, range(4 * (c - 2), 4 * (c - 1)))
            variances(range(NB))
            reciprocal_root(rstd, 0, slice(0, NB))
            e.wait_ge(s.mod_cols, 1)
            st.link(e.tensor_copy(mod_col[:, :, :].rearrange("p m k -> p (m k)"), psy[:, 0, 0:4 * KT]))
            for m in (1, 3):
                st.link(e.tensor_scalar(mod_col[:, m, :], mod_col[:, m, :], 1.0, None, ALU.add))
            assert st.count == DVE_STEPS["setup"], ("setup", st.count)

            with e.Fori(0, HALVES) as h:
                st.base, st.count = h * DVE_STEPS["half"] + DVE_STEPS["setup"], 0

                def normalise(which, src, b):
                    n = (2 * h + which) * NB + b
                    if b >= 2:
                        e.wait_ge(s.tp, n - 1)
                    e.tensor_scalar(xn[:, b % 2, :], src[:, b, :], mv[:, b, 0:1], rstd[:, b:b + 1],
                                    ALU.subtract, ALU.mult).then_inc(s.xn, 1)

                def round_h(which, b):
                    e.wait_ge(s.h32, (2 * h + which) * NB + b + 1)
                    e.tensor_copy(ht_hi[:, :, b * P:(b + 1) * P], h32[b % 4]).then_inc(s.ht_up, 1)

                edge(e, h, 1)
                for b in range(NB):
                    normalise(0, x_ln, b)
                    if b >= 2:
                        round_h(0, b - 2)
                for b in range(NB - 2, NB):
                    round_h(0, b)

                def tap(j, k):
                    m = h * TILES + j
                    raw, dst = raw_of(j), conv_of(j)
                    if k == 0:
                        e.wait_ge(s.tap0, m + 1)
                    else:
                        e.wait_ge(s.tap_k, 2 * m + k)
                    e.scalar_tensor_tensor(
                        out=dst[:, :], in0=raw[:, k:k + TH],
                        scalar=conv_w[:, bass.ds(j, 1), k:k + 1].rearrange("p a k -> p (a k)"),
                        in1=dst[:, :], op0=ALU.mult, op1=ALU.add).then_inc(s.tap_k if k < TAPS - 2 else s.taps, 1)

                def silu_x(j, dst):
                    m = h * TILES + j
                    e.wait_ge(s.thc, m + 1)
                    src = conv_of(j)
                    e.scalar_tensor_tensor(out=dst, in0=conv_th[:, :], scalar=1.0, in1=src[:, :],
                                           op0=ALU.add, op1=ALU.mult).then_inc(s.xs, 1)

                v, ab, ee, uu, lg, d, zero = dt_v, dt_ab, dt_ee, dt_uu, dt_lg, dt_d, dt_zero
                e.wait_ge(s.dt_tp, h + 1)
                st.link(e.tensor_tensor(v.rearrange("p (b k) -> p b k", b=NB),
                                        pso[:, 0, :].rearrange("p (b k) -> p b k", b=NB),
                                        dt_bias[:, :].unsqueeze(1).broadcast_to([P, NB, HEADS]), ALU.add))
                e.scalar_tensor_tensor(out=ab, in0=v, scalar=-1.0, in1=v, op0=ALU.mult, op1=ALU.max) \
                    .then_inc(s.dt_abs, 1)
                e.wait_ge(s.dt_exp, h + 1)
                e.tensor_scalar(uu, ee, 1.0, None, ALU.add).then_inc(s.dt_u, 1)
                e.wait_ge(s.dt_u, h + 1)
                st.link(e.tensor_scalar(d, uu, -1.0, None, ALU.add))
                st.link(e.tensor_scalar(zero, d, 0.0, None, ALU.is_equal))
                st.link(e.tensor_tensor(d, d, zero, ALU.add))
                st.mark(e.reciprocal(d, d))
                tap(0, 0)
                st.sync()
                st.link(e.tensor_tensor(d, d, ee, ALU.mult))
                e.wait_ge(s.dt_ln, h + 1)
                st.link(e.tensor_tensor(d, d, lg, ALU.mult))
                st.link(e.tensor_tensor(zero, zero, ee, ALU.mult))
                st.link(e.tensor_tensor(d, d, zero, ALU.add))
                st.link(e.scalar_tensor_tensor(out=d, in0=v, scalar=0.0, in1=d, op0=ALU.max, op1=ALU.add))
                st.link(e.tensor_scalar(flat(dt), d, 0.0, DT_MAX, ALU.max, ALU.min))
                e.scalar_tensor_tensor(out=dt_end[:, :, :], in0=dt[:, :, :], scalar=-1.0,
                                       in1=exp_a[:, :].unsqueeze(1).broadcast_to([P, NB, HEADS]),
                                       op0=ALU.mult, op1=ALU.mult).then_inc(s.dta, 1)
                tap(0, 1)
                tap(0, 2)
                e.wait_ge(s.cs_mm, h + 1)
                e.tensor_copy(flat(cs), psy[:, 0, :]).then_inc(s.cs_sb, 1)
                e.wait_ge(s.cs_sb, h + 1)
                st.link(e.tensor_tensor(flat(dt_end), psy[:, 1, :], flat(cs), ALU.subtract))
                e.tensor_scalar(flat(dt_end), flat(dt_end), 0.0, None, ALU.min).then_inc(s.csm, 1)
                silu_x(0, b_t[:, :])
                for k in range(TAPS - 1):
                    tap(1, k)
                e.wait_ge(s.dec, 2 * h + 2)
                e.tensor_tensor(flat(dt_end), flat(dt_end), flat(dt), ALU.mult)
                silu_x(1, c_t[:, :])
                for k in range(TAPS - 1):
                    tap(2, k)
                e.wait_ge(s.cb_mm, h + 1)
                e.tensor_tensor(cb[:, :, :], pst_b[:, :, :], tri[:, :].unsqueeze(1).broadcast_to([P, NB, P]),
                                ALU.mult)
                silu_x(2, xs[:, :])
                edge(e, h, 2)

                def accumulate(n, blocks, fresh=False):
                    for b in blocks:
                        e.wait_ge(s.op, START + NB * n + b + 1)
                        if fresh:
                            ins = e.tensor_copy(acc[:, b, :], pso[:, b % 2, :])
                        else:
                            ins = e.tensor_tensor(acc[:, b, :], pso[:, b % 2, :], acc[:, b, :], ALU.add)
                        ins.then_inc(s.oacc, 1)

                def heads(table, i, blocks=NB):
                    return table[:, :, bass.ds(2 * i, 2)].unsqueeze(3).broadcast_to([P, NB, 2, HEAD_P])

                four = "p b (r q) -> p b r q"

                def combine(i, q):
                    n = h * PAIRS + i
                    c = slice(q * 512, q * 512 + 512)
                    if q == 0:
                        e.wait_ge(s.erow_in, 32 * (n + 1))
                    e.wait_ge(s.yp, START + 2 * n + q + 1)
                    if not (isinstance(i, int) and i == 0):
                        e.wait_ge(s.ssq, START + 2 * n - 1 + q)
                    st.link(e.tensor_tensor(g[:, c], psy[:, 1, :], e_row[:, c], ALU.mult))
                    e.tensor_tensor(g[:, c], psy[:, 0, :], g[:, c], ALU.add).then_inc(s.y_read, 1)

                def gate(i, q):
                    n = h * PAIRS + i
                    c = slice(q * 512, q * 512 + 512)
                    e.wait_ge(s.y_skip, START + 2 * n + q + 1)
                    e.tensor_tensor(g[:, c], g[:, c], sz[:, c], ALU.mult).then_inc(s.g_r, 1)

                def decayed_x(i):
                    e.wait_ge(s.xT, h * PAIRS + i + 1)
                    e.tensor_tensor(xd[:, :, :].rearrange(four, r=2), pst_b[:, :, :].rearrange(four, r=2),
                                    heads(dt_end, i), ALU.mult).then_inc(s.xd_r, 1)

                def pair(i, parity, first=False, group=None, fresh=False, convolves=True):
                    n = h * PAIRS + i

                    def take(b):
                        if group is not None:
                            accumulate(h * GROUPS + group, [4 * parity + b], fresh)

                    def state(b):
                        for r in range(2):
                            hp = slice(r * HEAD_P, (r + 1) * HEAD_P)
                            dst = s_in[:, b + 1, hp] if b < NB - 1 else \
                                carry[:, bass.ds(i, 1), hp].rearrange("p a n -> p (a n)")
                            ins = e.scalar_tensor_tensor(out=dst, in0=s_in[:, b, hp],
                                                         scalar=e_last[:, b, bass.ds(2 * i + r, 1)],
                                                         in1=pst_b[:, b, hp], op0=ALU.mult, op1=ALU.add)
                            if b < NB - 1:
                                st.mark(ins)
                        if b == NB - 1:
                            ins.then_inc(s.sin, 1)

                    def decay(r):
                        e.wait_ge(s.ex, 2 * n + r + 1)
                        e.tensor_tensor(mt[:, r, :], cs_row[:, r, :], cb[:, :, :].rearrange("p b t -> p (b t)"),
                                        ALU.mult).then_inc(s.mt_r, 1)

                    def silu_z(q):
                        c = slice(q * 512, q * 512 + 512)
                        if not first:
                            e.wait_ge(s.g_r, 2 * n - 1 + q)
                        e.wait_ge(s.thz, 2 * n + q + 1)
                        e.scalar_tensor_tensor(out=sz[:, c], in0=z_th[:, c], scalar=1.0, in1=psx[:, q, :],
                                               op0=ALU.add, op1=ALU.mult).then_inc(s.szr, 1)

                    e.wait_ge(s.yp, START + 2 * n)
                    e.tensor_tensor(xdt[:, :, :].rearrange(four, r=2), pst_b[:, :, :].rearrange(four, r=2),
                                    heads(dt, i), ALU.mult).then_inc(s.xdt_r, 1)
                    st.mark(e.tensor_copy(s_in[:, 0, :], carry[:, bass.ds(i, 1), :].rearrange("p a n -> p (a n)")))
                    if not first:
                        combine(i - 1, 1)
                        gate(i - 1, 0)
                    if convolves:
                        tap(i + 3, 0)
                    if first:
                        for q in range(2):
                            silu_z(q)
                    st.sync()
                    e.wait_ge(s.st, n + 1)
                    state(0)
                    if convolves:
                        tap(i + 3, 1)
                    st.sync()
                    state(1)
                    if not first:
                        silu_z(0)
                    st.sync()
                    state(2)
                    if not first:
                        gate(i - 1, 1)
                    st.sync()
                    state(3)
                    if not first:
                        silu_z(1)
                    st.sync()
                    state(4)
                    decay(0)
                    st.sync()
                    state(5)
                    take(0)
                    take(1)
                    st.sync()
                    state(6)
                    decay(1)
                    st.sync()
                    state(7)
                    if convolves:
                        tap(i + 3, 2)
                    take(2)
                    take(3)
                    if convolves:
                        e.wait_ge(s.x_skip, n + 1)
                        silu_x(i + 3, xs[:, :])
                    combine(i, 0)
                    if convolves:
                        decayed_x(i + 1)

                decayed_x(0)
                pair(0, 0, first=True)
                pair(1, 1)
                pair(2, 0, group=0, fresh=True)
                pair(3, 1, group=0, fresh=True)
                at, base = st.count, st.base
                with e.Fori(2, GROUPS - 1) as k:
                    st.base, st.count = base + (k - 2) * DVE_STEPS["pair"] + at, 0
                    pair(2 * k, 0, group=k - 1)
                    pair(2 * k + 1, 1, group=k - 1)
                    assert st.count == DVE_STEPS["pair"], ("pair", st.count)
                st.base, st.count = base, at + (GROUPS - 3) * DVE_STEPS["pair"]
                pair(PAIRS - 2, 0, group=GROUPS - 2)
                pair(PAIRS - 1, 1, group=GROUPS - 2, convolves=False)
                gate(PAIRS - 1, 0)
                combine(PAIRS - 1, 1)
                gate(PAIRS - 1, 1)
                last = h * GROUPS + GROUPS - 1
                accumulate(last, range(4))
                e.wait_ge(s.ss_mm, h + 1)
                e.tensor_scalar(var[:, :], psy[:, 0, 0:NB], 1.0 / (4 * INTER), RMS_EPS, ALU.mult, ALU.add) \
                    .then_inc(s.var_r, 1)
                reciprocal_root(rms, 1, slice(0, NB))
                st.link(e.tensor_scalar(rms[:, :], rms[:, :], 0.5, None, ALU.mult))

                def scale_mixer(b):
                    e.scalar_tensor_tensor(out=acc[:, b, :], in0=acc[:, b, :], scalar=rms[:, b:b + 1],
                                           in1=gate_a[:, :], op0=ALU.mult, op1=ALU.mult).then_inc(s.res, 1)

                e.wait_ge(s.oacc, START + NB * last + 4)
                for b in range(4):
                    scale_mixer(b)
                    accumulate(last, [b + 4])
                first, rest = range(4), range(4, NB)
                e.wait_ge(s.oacc, START + NB * last + NB)
                for b in rest:
                    scale_mixer(b)
                e.wait_ge(s.x2, h * NB + 4)
                statistics(acc, first)
                variances(first)
                reciprocal_root(rstd, 2, slice(0, 4))
                normalise(1, acc, 0)
                normalise(1, acc, 1)
                e.wait_ge(s.x2, h * NB + NB)
                statistics(acc, rest)
                normalise(1, acc, 2)
                round_h(1, 0)
                variances(rest)
                normalise(1, acc, 3)
                round_h(1, 1)
                reciprocal_root(rstd, 3, slice(4, 8))
                for b in rest:
                    normalise(1, acc, b)
                    round_h(1, b - 2)
                for b in range(NB - 2, NB):
                    round_h(1, b)

                def take_down(n):
                    for b in range(NB):
                        e.wait_ge(s.fp, START + NB * n + b + 1)
                        e.tensor_tensor(acc[:, b, :], down_banks[b % 4], acc[:, b, :], ALU.add).then_inc(s.facc, 1)

                def ffn(t, first=False):
                    n = h * FT + t
                    e.wait_ge(s.wd_in, 16 * (n + 1))
                    e.tensor_tensor(w_raw[:, O, :], w_raw[:, O, :], gate_b[:, :], ALU.mult).then_inc(s.wd_sc, 1)
                    e.wait_ge(s.thg, n + 1)
                    st.link(e.scalar_tensor_tensor(out=conv_th[:, :], in0=conv_th[:, :], scalar=1.0, in1=conv[:, :],
                                                   op0=ALU.add, op1=ALU.mult))
                    e.wait_ge(s.up, START + n + 1)
                    e.wait_ge(s.hdlo, START + n)
                    e.scalar_tensor_tensor(out=g[:, :], in0=pst[:, :, :].rearrange("p a n -> p (a n)"),
                                           scalar=ffn_us[:, bass.ds(t, 1)], in1=conv_th[:, :],
                                           op0=ALU.mult, op1=ALU.mult).then_inc(s.hd, 1)
                    if not first:
                        take_down(n - 1)

                ffn(0, True)
                at, base = st.count, st.base
                with e.Fori(1, FT - 1) as t:
                    st.base, st.count = base + (t - 1) * DVE_STEPS["ffn"] + at, 0
                    ffn(t)
                    assert st.count == DVE_STEPS["ffn"], ("ffn", st.count)
                st.base, st.count = base, at + (FT - 2) * DVE_STEPS["ffn"]
                ffn(FT - 1)
                for k in range(2):
                    e.wait_ge(s.x_in[k], 16 * HALVES)
                    statistics(x_ln, range(4 * k, 4 * k + 4))
                variances(range(NB))
                take_down(h * FT + FT - 1)
                reciprocal_root(rstd, 4, slice(0, NB))
                assert st.count == DVE_STEPS["half"], ("half", st.count)

        @block.gpsimd
        def _(e):
            start_counters(e, s.wx_lo, s.wz_lo, s.wo_lo, s.wg_lo, s.wu_lo, s.wd_lo, s.ssq, s.hdlo, s.y_skip, s.seg)
            e.memset(ident[:, :], 0.0).then_inc(s.const_ok, 1)
            e.memset(tri[:, :], 1.0).then_inc(s.const_ok, 1)
            e.wait_ge(s.const_ok, 3)
            e.affine_select(out=ident[:, :], in_=ident[:, :], compare_op=ALU.not_equal, fill=1.0, base=0,
                            pattern=[[-1, P]], channel_multiplier=1).then_inc(s.const_ok, 1)
            e.affine_select(out=tri[:, :], in_=tri[:, :], compare_op=ALU.is_ge, fill=0.0, base=0,
                            pattern=[[1, P]], channel_multiplier=-1).then_inc(s.const_ok, 1)
            with e.Fori(0, HALVES) as h:
                edge(e, h, 1)
                e.memset(sumsq[:, :], 0.0)

                def rest_h(which):
                    for b in range(NB):
                        e.wait_ge(s.ht_up, (2 * h + which) * NB + b + 1)
                        t = slice(b * P, (b + 1) * P)
                        e.tensor_tensor(ht_lo[:, :, t], h32[b % 4], ht_hi[:, :, t].bitcast(F32), ALU.subtract) \
                            .then_inc(s.ht, 1)

                def low(k, hi_done, count, done, to=None):
                    to = k if to is None else to
                    e.wait_ge(hi_done, count)
                    e.tensor_tensor(w_lo[:, to, :], w_raw[:, k, :], w_hi[:, to, :].bitcast(F32), ALU.subtract) \
                        .then_inc(done, 1)

                for j in range(3):
                    low(j, s.wx_hi, h * TILES + j + 1, s.wx_lo, x_slots[j])
                rest_h(0)
                low(X, s.wx_hi, h * TILES + 4, s.wx_lo)
                low(Z, s.wz_hi, h * PAIRS + 1, s.wz_lo)

                def blocks(row):
                    return row.rearrange("p (b t) -> p b t", b=NB)

                def cs_s(i, r):
                    return cs[:, :, bass.ds(2 * i + r, 1)].broadcast_to([P, NB, P])

                def exponents(i, r):
                    e.wait_ge(s.csrow_in[r], 16 * (h * PAIRS + i + 1))
                    e.tensor_tensor(blocks(cs_row[:, r, :]), blocks(cs_row[:, r, :]), cs_s(i, r),
                                    ALU.subtract).then_inc(s.seg, 1)

                exponents(0, 0)
                edge(e, h, 2)

                def skip(i, q):
                    n = h * PAIRS + i
                    c = slice(q * 512, q * 512 + 512)
                    if q == 0:
                        e.wait_ge(s.x_skip, n + 1)
                    e.wait_ge(s.y_read, START + 2 * n + q + 1)
                    e.tensor_tensor(g[:, c], g[:, c], x_skip[:, c], ALU.add).then_inc(s.y_skip, 1)

                def rest(i, parity, q):
                    n = h * PAIRS + i
                    c = slice(q * 512, q * 512 + 512)
                    e.wait_ge(s.ghi, 2 * n + q + 1)
                    e.tensor_tensor(g_lo[:, parity, c], g[:, c], g_hi[:, parity, c].bitcast(F32), ALU.subtract) \
                        .then_inc(s.glo, 1)

                def add_squares(i, q):
                    n = h * PAIRS + i
                    c = slice(q * 512, q * 512 + 512)
                    e.wait_ge(s.sqr, 2 * n + q + 1)
                    e.tensor_tensor(sumsq[:, c], sumsq[:, c], g[:, c], ALU.add).then_inc(s.ssq, 1)

                def pair(i, parity, first=False, convolves=True, projects=True):
                    n = h * PAIRS + i
                    if not first:
                        rest(i - 1, 1 - parity, 0)
                        skip(i - 1, 1)
                    if projects:
                        low(X, s.wx_hi, h * TILES + i + 5, s.wx_lo)
                    exponents(i, 1)
                    if not first:
                        if parity == 0:
                            rest(i - 1, 1, 1)
                        add_squares(i - 1, 0)
                        if parity == 0:
                            add_squares(i - 1, 1)
                    if convolves:
                        low(Z, s.wz_hi, n + 2, s.wz_lo)
                    if parity == 1:
                        rest(i - 1, 0, 1)
                        low(O, s.wo_hi, n, s.wo_lo)
                        if not convolves:
                            low(O + 1, s.wo_hi, n + 1, s.wo_lo)
                        else:
                            add_squares(i - 1, 1)
                    skip(i, 0)
                    if parity == 1:
                        if not convolves:
                            add_squares(i - 1, 1)
                        else:
                            low(O + 1, s.wo_hi, n + 1, s.wo_lo)
                    if convolves:
                        exponents(i + 1, 0)

                pair(0, 0, first=True)
                pair(1, 1)
                with e.Fori(1, GROUPS - 1) as k:
                    pair(2 * k, 0)
                    pair(2 * k + 1, 1)
                pair(PAIRS - 2, 0, projects=False)
                pair(PAIRS - 1, 1, convolves=False, projects=False)
                rest(PAIRS - 1, 1, 0)
                skip(PAIRS - 1, 1)
                rest(PAIRS - 1, 1, 1)
                for q in range(2):
                    add_squares(PAIRS - 1, q)

                def low_in(t):
                    low(Z, s.wg_hi, h * FT + t + 1, s.wg_lo)
                    low(X, s.wu_hi, h * FT + t + 1, s.wu_lo)

                low_in(0)
                for b in range(NB):
                    if b % 4 == 0:
                        e.wait_ge(s.xres_in[b // 4], 16 * (h + 1))
                    e.wait_ge(s.res, h * NB + b + 1)
                    e.tensor_tensor(acc[:, b, :], acc[:, b, :], x_res[:, b, :], ALU.add).then_inc(s.x2, 1)
                rest_h(1)

                def ffn(t, u, last=False):
                    n = h * FT + t
                    if not last:
                        low_in(t + 1)
                    e.wait_ge(s.hdhi, n + 1)
                    e.tensor_tensor(g_lo[:, u, :], g[:, :], g_hi[:, u, :].bitcast(F32), ALU.subtract) \
                        .then_inc(s.hdlo, 1)
                    low(O, s.wd_hi, n + 1, s.wd_lo, O + u)

                ffn(0, 0)
                with e.Fori(0, (FT - 3) // 2) as k:
                    ffn(2 * k + 1, 1)
                    ffn(2 * k + 2, 0)
                ffn(FT - 2, 1)
                ffn(FT - 1, 0, last=True)


def tiles(w, n):
    return np.ascontiguousarray(w.reshape(KT, P, n, P).transpose(2, 1, 0, 3).reshape(n, P, KT * P))


def kernel(**inputs):
    import concourse.bacc as bacc
    from concourse.bass_utils import run_bass_kernel_spmd

    v = {k: np.asarray(x) for k, x in inputs.items()}
    w_in = v["L0_attn_W_in"]
    conv_dim = INTER + 2 * STATE
    w_z, w_xbc, w_dt = w_in[:, :INTER], w_in[:, INTER:INTER + conv_dim], w_in[:, INTER + conv_dim:]

    def bc_first(t):
        return np.concatenate([t[..., INTER:], t[..., :INTER]], axis=-1)

    def col(t, n):
        return np.ascontiguousarray(t.reshape(n, P).T)

    arrays = {
        "x": v["L0_attn_hidden_states"].reshape(TOKENS, HID),
        "wx": tiles(bc_first(w_xbc), TILES),
        "wz": tiles(w_z, PAIRS),
        "wdt": w_dt.reshape(KT, P, HEADS).transpose(1, 0, 2),
        "wo": v["L0_attn_W_out"].reshape(PAIRS, P, HID),
        "conv_w": bc_first(v["L0_attn_conv_w"]).reshape(TAPS, TILES, P).transpose(2, 1, 0),
        "conv_b": col(bc_first(v["L0_attn_conv_b"]), TILES),
        "dt_bias": v["L0_attn_dt_bias"], "a_log": v["L0_attn_A_log"],
        "d": v["L0_attn_D"].reshape(PAIRS, 2).T,
        "norm_w": col(v["L0_attn_norm_weight"], PAIRS),
        "wg": tiles(v["L0_ffn_gate_w"].T, FT), "wu": tiles(v["L0_ffn_up_w"].T, FT),
        "wd": v["L0_ffn_down_w"].T.reshape(FT, P, HID),
        "gate_s": col(v["L0_ffn_gate_s"], FT), "up_s": col(v["L0_ffn_up_s"], FT),
        "down_s": v["L0_ffn_down_s"],
        "c": col(v["L0_c"], KT), "wmod": v["L0_wmod"],
    }
    arrays = {f"in_{k}": np.ascontiguousarray(t) for k, t in arrays.items()}
    nc = bacc.Bacc("TRN2", target_bir_lowering=False, num_devices=1)
    aps = {k[3:]: nc.dram_tensor(k, t.shape, mybir.dt.from_np(t.dtype), kind="ExternalInput").ap()
           for k, t in arrays.items()}
    out = nc.dram_tensor("out", (TOKENS, HID), F32, kind="ExternalOutput").ap()
    build(nc, aps, out)
    r = run_bass_kernel_spmd(nc, [arrays], core_ids=[0])
    return np.asarray(r.results[0]["out"]).reshape(1, TOKENS, HID)
```
